# Optimizing a Trainium2 kernel written in Bass

```python
import numpy as np
import jax
import jax.numpy as jnp

def _softmax(x, axis=-1):
    return jax.nn.softmax(x, axis=axis)

def _gelu(x):
    return jax.nn.gelu(x, approximate=True)

def _silu(x):
    return jax.nn.silu(x)

def _sigmoid(x):
    return jax.nn.sigmoid(x)

def _layernorm(x, axis=-1, eps=1e-05):
    m = jnp.mean(x, axis=axis, keepdims=True)
    v = jnp.var(x, axis=axis, keepdims=True)
    return (x - m) / jnp.sqrt(v + eps)

def _scatter_add(tgt, idx, src, axis=0):
    return tgt.at[idx].add(src)

def _segment_sum(src, seg, n):
    return jax.ops.segment_sum(src, seg, n)
kernel_name = 'mk_gnn_resnorm_d1_gnn_r8_991098'

def setup_inputs(seed: int=0):
    np.random.seed(seed)
    _w = jnp.asarray

    def _rec_inputs():
        import jax
        import jax.numpy as jnp
        _gk = jax.random.key(seed)
        x = -0.0008691 + 1 * jax.random.normal(jax.random.fold_in(_gk, 1), (12500, 128), jnp.float32)
        _s = jax.random.randint(jax.random.fold_in(_gk, 2), (200000,), 0, 12500, jnp.int32)
        _d = jax.random.randint(jax.random.fold_in(_gk, 3), (200000,), 0, 12500, jnp.int32)
        _loop = jnp.arange(12500, dtype=jnp.int32)
        src = jnp.concatenate([_s, _d, _loop])
        dst = jnp.concatenate([_d, _s, _loop])
        _o = jnp.argsort(dst, stable=True)
        src = src[_o]
        dst = dst[_o]
        edge_attr_4 = -0.000149047 + 1.00006 * jax.random.normal(jax.random.fold_in(_gk, 12), (412500, 4), jnp.float32)
        edge_attr_8 = jax.random.uniform(jax.random.fold_in(_gk, 13), (412500, 8), jnp.float32, 0.0, 0.999999)
        return (x, src, dst, edge_attr_4, edge_attr_8)
    x, src, dst, edge_attr_4, edge_attr_8 = _rec_inputs()

    def _L0_gnn_setup():
        import jax, jax.numpy as jnp
        import numpy as np
        N_NODES = 1250
        N_EDGES = 40000
        MUL = 32
        RADIAL = 8
        HID = 64
        NUM_NEIGHBORS = 32.0
        MIX = np.pi / 8.0
        INV_SQRT2 = 1.0 / np.sqrt(2.0)
        INV_SQRT3 = 1.0 / np.sqrt(3.0)

        def _forward(node_input, edge_attr, edge_scalar_attr, W1_0e, W1_1o, W_mlp1, W_mlp2, Wp_00, Wp_01, Wp_10, Wp_11, W2_0e, W2_1o, edge_src, edge_dst):
            N = node_input.shape[0]
            x0 = node_input[:, :MUL]
            x1 = node_input[:, MUL:].reshape(N, MUL, 3)
            f0 = x0 @ W1_0e / np.sqrt(MUL)
            f1 = jnp.einsum('nui,uw->nwi', x1, W1_1o) / np.sqrt(MUL)
            feat0, self0 = (f0[:, :MUL], f0[:, MUL:])
            feat1, self1 = (f1[:, :MUL], f1[:, MUL:])
            e0 = feat0[edge_src]
            e1 = feat1[edge_src]
            ea0 = edge_attr[:, :1]
            ea1 = edge_attr[:, 1:4]
            h = jax.nn.gelu(edge_scalar_attr @ W_mlp1 / np.sqrt(RADIAL))
            h = jax.nn.gelu(h @ W_mlp2 / np.sqrt(HID))
            w00 = h @ Wp_00
            w01 = h @ Wp_01
            w10 = h @ Wp_10
            w11 = h @ Wp_11
            out0_a = w00 * e0 * ea0
            out0_b = w11 * jnp.sum(e1 * ea1[:, None, :], -1) * INV_SQRT3
            out1_a = (w01 * e0)[:, :, None] * ea1[:, None, :]
            out1_b = w10[:, :, None] * e1 * ea0[:, :, None]
            mid0 = jnp.concatenate([out0_a, out0_b], axis=1) * INV_SQRT2
            mid1 = jnp.concatenate([out1_a, out1_b], axis=1) * INV_SQRT2
            n0 = jax.ops.segment_sum(mid0, edge_dst, num_segments=N) / np.sqrt(NUM_NEIGHBORS)
            n1 = jax.ops.segment_sum(mid1, edge_dst, num_segments=N) / np.sqrt(NUM_NEIGHBORS)
            conv0 = n0 @ W2_0e / np.sqrt(2 * MUL)
            conv1 = jnp.einsum('nui,uw->nwi', n1, W2_1o) / np.sqrt(2 * MUL)
            c, s = (np.cos(MIX), np.sin(MIX))
            y0 = c * self0 + s * conv0
            y1 = c * self1 + s * conv1
            return jnp.concatenate([y0, y1.reshape(N, MUL * 3)], axis=1)
        key = jax.random.key(seed)
        ks = jax.random.split(key, 16)
        inp = {'node_input': jax.random.normal(ks[0], (N_NODES, 4 * MUL), jnp.float32), 'edge_attr': jax.random.normal(ks[1], (N_EDGES, 4), jnp.float32), 'edge_scalar_attr': jax.random.uniform(ks[2], (N_EDGES, RADIAL), jnp.float32), 'W1_0e': jax.random.normal(ks[3], (MUL, 2 * MUL), jnp.float32), 'W1_1o': jax.random.normal(ks[4], (MUL, 2 * MUL), jnp.float32), 'W_mlp1': jax.random.normal(ks[5], (RADIAL, HID), jnp.float32), 'W_mlp2': jax.random.normal(ks[6], (HID, HID), jnp.float32), 'Wp_00': jax.random.normal(ks[7], (HID, MUL), jnp.float32), 'Wp_01': jax.random.normal(ks[8], (HID, MUL), jnp.float32), 'Wp_10': jax.random.normal(ks[9], (HID, MUL), jnp.float32), 'Wp_11': jax.random.normal(ks[10], (HID, MUL), jnp.float32), 'W2_0e': jax.random.normal(ks[11], (2 * MUL, MUL), jnp.float32), 'W2_1o': jax.random.normal(ks[12], (2 * MUL, MUL), jnp.float32), 'edge_src': jax.random.randint(ks[13], (N_EDGES,), 0, N_NODES, jnp.int32), 'edge_dst': jax.random.randint(ks[14], (N_EDGES,), 0, N_NODES, jnp.int32)}
        return inp
    _L0_gnn_all = _L0_gnn_setup()
    _L0_gnn_in = {k: v for k, v in _L0_gnn_all.items() if k in ('W1_0e', 'W1_1o', 'W_mlp1', 'W_mlp2', 'Wp_00', 'Wp_01', 'Wp_10', 'Wp_11', 'W2_0e', 'W2_1o')}
    del _L0_gnn_all
    return {'x': x, 'src': src, 'dst': dst, 'edge_attr_4': edge_attr_4, 'edge_attr_8': edge_attr_8, 'L0_gnn_W1_0e': _L0_gnn_in['W1_0e'], 'L0_gnn_W1_1o': _L0_gnn_in['W1_1o'], 'L0_gnn_W_mlp1': _L0_gnn_in['W_mlp1'], 'L0_gnn_W_mlp2': _L0_gnn_in['W_mlp2'], 'L0_gnn_Wp_00': _L0_gnn_in['Wp_00'], 'L0_gnn_Wp_01': _L0_gnn_in['Wp_01'], 'L0_gnn_Wp_10': _L0_gnn_in['Wp_10'], 'L0_gnn_Wp_11': _L0_gnn_in['Wp_11'], 'L0_gnn_W2_0e': _L0_gnn_in['W2_0e'], 'L0_gnn_W2_1o': _L0_gnn_in['W2_1o']}

def reference(x, src, dst, edge_attr_4, edge_attr_8, L0_gnn_W1_0e, L0_gnn_W1_1o, L0_gnn_W_mlp1, L0_gnn_W_mlp2, L0_gnn_Wp_00, L0_gnn_Wp_01, L0_gnn_Wp_10, L0_gnn_Wp_11, L0_gnn_W2_0e, L0_gnn_W2_1o):
    import jax
    import jax.numpy as jnp

    def _L0_gnn_ref(node_input, edge_attr, edge_scalar_attr, W1_0e, W1_1o, W_mlp1, W_mlp2, Wp_00, Wp_01, Wp_10, Wp_11, W2_0e, W2_1o, edge_src, edge_dst):
        import jax, jax.numpy as jnp
        import numpy as np
        N_NODES = 1250
        N_EDGES = 40000
        MUL = 32
        RADIAL = 8
        HID = 64
        NUM_NEIGHBORS = 32.0
        MIX = np.pi / 8.0
        INV_SQRT2 = 1.0 / np.sqrt(2.0)
        INV_SQRT3 = 1.0 / np.sqrt(3.0)

        def _forward(node_input, edge_attr, edge_scalar_attr, W1_0e, W1_1o, W_mlp1, W_mlp2, Wp_00, Wp_01, Wp_10, Wp_11, W2_0e, W2_1o, edge_src, edge_dst):
            N = node_input.shape[0]
            x0 = node_input[:, :MUL]
            x1 = node_input[:, MUL:].reshape(N, MUL, 3)
            f0 = x0 @ W1_0e / np.sqrt(MUL)
            f1 = jnp.einsum('nui,uw->nwi', x1, W1_1o) / np.sqrt(MUL)
            feat0, self0 = (f0[:, :MUL], f0[:, MUL:])
            feat1, self1 = (f1[:, :MUL], f1[:, MUL:])
            e0 = feat0[edge_src]
            e1 = feat1[edge_src]
            ea0 = edge_attr[:, :1]
            ea1 = edge_attr[:, 1:4]
            h = jax.nn.gelu(edge_scalar_attr @ W_mlp1 / np.sqrt(RADIAL))
            h = jax.nn.gelu(h @ W_mlp2 / np.sqrt(HID))
            w00 = h @ Wp_00
            w01 = h @ Wp_01
            w10 = h @ Wp_10
            w11 = h @ Wp_11
            out0_a = w00 * e0 * ea0
            out0_b = w11 * jnp.sum(e1 * ea1[:, None, :], -1) * INV_SQRT3
            out1_a = (w01 * e0)[:, :, None] * ea1[:, None, :]
            out1_b = w10[:, :, None] * e1 * ea0[:, :, None]
            mid0 = jnp.concatenate([out0_a, out0_b], axis=1) * INV_SQRT2
            mid1 = jnp.concatenate([out1_a, out1_b], axis=1) * INV_SQRT2
            n0 = jax.ops.segment_sum(mid0, edge_dst, num_segments=N) / np.sqrt(NUM_NEIGHBORS)
            n1 = jax.ops.segment_sum(mid1, edge_dst, num_segments=N) / np.sqrt(NUM_NEIGHBORS)
            conv0 = n0 @ W2_0e / np.sqrt(2 * MUL)
            conv1 = jnp.einsum('nui,uw->nwi', n1, W2_1o) / np.sqrt(2 * MUL)
            c, s = (np.cos(MIX), np.sin(MIX))
            y0 = c * self0 + s * conv0
            y1 = c * self1 + s * conv1
            return jnp.concatenate([y0, y1.reshape(N, MUL * 3)], axis=1)
        return _forward(node_input, edge_attr, edge_scalar_attr, W1_0e, W1_1o, W_mlp1, W_mlp2, Wp_00, Wp_01, Wp_10, Wp_11, W2_0e, W2_1o, edge_src, edge_dst)
    x = _layernorm(x + _L0_gnn_ref(x, edge_attr_4, edge_attr_8, L0_gnn_W1_0e, L0_gnn_W1_1o, L0_gnn_W_mlp1, L0_gnn_W_mlp2, L0_gnn_Wp_00, L0_gnn_Wp_01, L0_gnn_Wp_10, L0_gnn_Wp_11, L0_gnn_W2_0e, L0_gnn_W2_1o, src, dst), axis=-1)
    return x

_drawn_inputs = setup_inputs


def setup_inputs(seed=0):
    import zlib

    import numpy as np

    out = dict(_drawn_inputs(seed))
    spreads = {}
    factors = {}
    for name, (base, spread) in spreads.items():
        noise = np.random.default_rng([zlib.crc32(name.encode()), seed]).standard_normal(out[name].shape)
        drawn = base * np.exp(spread * noise) if base else spread * noise
        out[name] = jnp.asarray(drawn.astype(out[name].dtype))
    for name, factor in factors.items():
        out[name] = (out[name] * factor).astype(out[name].dtype)
    return out
```

```python
import math

import concourse.bass as bass
from concourse import mybir
from contextlib import ExitStack

FP32 = mybir.dt.float32
INT32 = mybir.dt.int32
INT16 = mybir.dt.int16
BF16 = mybir.dt.bfloat16
ALU = mybir.AluOpType
ACT = mybir.ActivationFunctionType
AXIS_X = mybir.AxisListType.X

NODES, FEAT, EDGES = 12500, 128, 412500
MUL, RADIAL, HID = 32, 8, 64
NODE_P = 125
NODE_J = NODES // NODE_P
BATCH = 4
NODE_BATCHES = NODE_J // BATCH
PIECE = 20
PIECES = NODE_J // PIECE
GROUP = 256
BLOCK = 2048
GROUPS = BLOCK // GROUP
TILES = BLOCK // 128
CHUNKS = 4
CT = TILES // CHUNKS
BLOCKS = -(-EDGES // BLOCK)
LAST_START = EDGES - BLOCK
OVERLAP = BLOCKS * BLOCK - EDGES
ALL_GROUPS = BLOCKS * GROUPS
ROWS = -(-ALL_GROUPS // 128)
WINDOW = 16
SLOTS = 4
QUADS = (BLOCKS - 2) // SLOTS
assert BLOCKS == 2 + SLOTS * QUADS

MIX = math.pi / 8.0
SELF_SCALE = math.cos(MIX) / math.sqrt(MUL)
FEAT_SCALE = 1.0 / math.sqrt(MUL)
CONV_SCALE = math.sin(MIX) / math.sqrt(2.0) / math.sqrt(32.0) / math.sqrt(2.0 * MUL)
INV_SQRT3 = 1.0 / math.sqrt(3.0)
EPS = 1e-05


def rows_of(c):
    return min(128, ALL_GROUPS - 128 * c)


def build_program(nc, x, src, dst, ea4, ea8, W1_0e, W1_1o, W_mlp1, W_mlp2, Wp, W2_0e, W2_1o, out):
    ctx = ExitStack()
    with ctx:
        def sb(name, shape, dt=FP32):
            return ctx.enter_context(nc.sbuf_tensor(name, shape, dt))

        def sem(name):
            return ctx.enter_context(nc.semaphore(name))

        table = nc.dram_tensor("feature_table", [NODES, FEAT], FP32, kind="Internal").ap()
        base_dram = nc.dram_tensor("group_bases", [ROWS, 128], INT32, kind="Internal").ap()

        acc = sb("acc", [128, NODES + WINDOW])
        ea_all = sb("ea_all", [128, ALL_GROUPS * 2 * 4])
        rel_all = sb("rel_all", [128, ALL_GROUPS * 2], BF16)
        src_all = sb("src_all", [128, (BLOCKS + 2) * TILES], INT16)
        gath = sb("gath", [128, SLOTS, TILES, FEAT])
        idx = sb("idx", [128, SLOTS, TILES], INT32)
        e8 = sb("e8", [128, SLOTS, 128])
        e8T = sb("e8T", [128, 128])
        zsb = sb("zsb", [128, GROUPS * 4 * WINDOW])
        ident = sb("ident", [128, 128])
        iota_i = sb("iota_i", [128, WINDOW], INT32)
        iota_w = sb("iota_w", [128, WINDOW], BF16)
        w1bd = sb("w1bd", [128, 8, 128])
        w2bd = sb("w2bd", [128, 128])
        wpbd = sb("wpbd", [128, 2 * 128])
        wfeat = sb("wfeat", [128, 128])
        winit = sb("winit", [128, 128])
        conv = sb("conv", [128, 4, 128])
        base_f = sb("base_f", [128, ROWS])
        relmax = sb("relmax", [128, ROWS + 1])
        base13 = sb("base13", [ROWS, 128], INT32)
        base_row = sb("base_row", [1, ROWS * 128], INT32)
        flag_i = sb("flag_i", [1, 8], INT32)
        stats = sb("stats", [128, 4, BATCH, 6])
        moments = sb("moments", [128, 4, BATCH, 2])
        rstd = sb("rstd", [128, 4, BATCH, 2])
        eps_col = sb("eps_col", [128, 1])

        work = sb("work", [128, 9216])
        prod = work[:, 0:4096].rearrange("p (c t f) -> p c t f", c=CHUNKS, t=CT)
        sel = work[:, 4096:6144].rearrange("p (b t k w) -> p b t k w", b=2, t=TILES, k=4)
        h1 = work[:, 6144:7168].rearrange("p (h n) -> p h n", h=2)
        h2 = work[:, 7168:9216].rearrange("p (b e a) -> p b e a", b=2, a=8)
        dst_rows = work[:, 0:ROWS * 256].rearrange("p (c e) -> p c e", c=ROWS)
        src_rows = work[:, ROWS * 256:2 * ROWS * 256].rearrange("p (c e) -> p c e", c=ROWS)
        ea_rows = work[:, 2 * ROWS * 256:2 * ROWS * 256 + 2048].rearrange("p (b e) -> p b e", b=2)
        assert 2 * ROWS * 256 + 2048 <= 9216
        wself_raw = zsb[:, 0:128]
        xT = e8[:, 0:SLOTS, :]
        x_rows = ea_all[0:NODE_P, 0:NODE_J * FEAT].rearrange("p (j d) -> p j d", d=FEAT)
        feat_rows = gath[0:NODE_P, :, :, :].rearrange("p s t f -> p (s t) f")[:, 0:2 * PIECE, :]\
            .rearrange("p (b j) f -> p b j f", b=2)
        sel01 = sb("sel01", [128, TILES, WINDOW])
        conv_stage = sb("conv_stage", [128, 4, 128])
        diag = work[:, 4096:5120].rearrange("p (t k n) -> p t k n", t=2, k=4)
        gen_z = work[:, 3072:4096].rearrange("p (t k n) -> p t k n", t=2, k=4)

        bank = [ctx.enter_context(nc.psum_tensor(f"bank{i}", [128, 512], FP32)) for i in range(8)]
        hid_ps = [bank[0], bank[1]]
        wgt_ps = [bank[2], bank[3], bank[4], bank[5]]
        z_ps = bank[6]
        t_ps = bank[0][:, 0:128]
        y_ps = bank[7][:, 0:128]

        s_node_w = sem("node_weights_in")
        s_x = [sem(f"x_in{i}") for i in range(PIECES)]
        s_rows = sem("index_rows_zeroed")
        s_dst = sem("dst_in")
        s_src = sem("src_in")
        s_ea = [sem(f"ea_in{i}") for i in range(2)]
        s_eaz = sem("ea_tail_zeroed")
        s_zero = sem("weights_zeroed")
        s_zero_node = sem("node_weights_zeroed")
        s_wts = sem("loop_weights_in")
        s_ident0 = sem("ident_zeroed")
        s_ident = sem("ident_ready")
        s_iota = sem("iota_ready")
        s_prep = sem("vector_chain")
        s_wnode = sem("node_weights_ready")
        s_xt = sem("x_transposed")
        s_xts = sem("x_transposed_copied")
        s_featp = sem("features_done")
        s_feats = sem("features_copied")
        s_initp = sem("init_done")
        s_inits = sem("init_copied")
        s_tab = [sem(f"table_stored{i}") for i in range(2)]
        s_src_f = sem("src_as_float")
        s_base = sem("bases_ready")
        s_small = sem("small_transposes_done")
        s_base13 = sem("bases_transposed")
        s_bd = sem("bases_in_dram")
        s_br = sem("bases_in_row")
        s_flag = sem("flag_ready")
        s_rt = sem("index_transposes_done")
        s_rts = sem("index_transposes_copied")
        s_et = sem("ea_transposes_done")
        s_ets = sem("ea_transposes_copied")
        s_conv = sem("conv_weights_ready")
        s_e8 = [sem(f"e8_in{i}") for i in range(SLOTS)]
        s_tr = sem("e8_transposed")
        s_e8T = sem("e8_transposed_copied")
        s_h1p = sem("layer1_done")
        s_h1 = sem("gelu1_done")
        s_h2p = sem("layer2_done")
        s_h2 = sem("gelu2_done")
        s_w = sem("radial_weights_done")
        s_idx = sem("indices_ready")
        s_g = [[sem(f"gathered{s}_{c}") for c in range(CHUNKS)] for s in range(SLOTS)]
        s_round = sem("gather_slot_seen_free")
        s_sel0 = sem("onehot_ready")
        s_sel = sem("selection_ready")
        s_prod = sem("products_ready")
        s_seg = sem("segments_summed")
        s_zc = sem("sums_copied")
        s_y = sem("conv_done")
        s_add = sem("window_added")
        s_gz = sem("general_sums_done")
        s_gzc = sem("general_sums_copied")
        s_gprod = sem("general_products_ready")
        s_gdiag = sem("general_diagonals_ready")
        s_gw = sem("general_weights_done")
        s_gy = sem("general_conv_done")
        s_gblk = sem("general_block_added")
        s_ft = sem("rows_transposed")
        s_var = sem("variance_ready")
        s_std = sem("std_ready")
        s_sc = sem("scale_ready")
        s_yr = sem("rows_normalised")
        s_out = sem("out_stored")

        x_v = x.rearrange("(p j) d -> p j d", j=NODE_J)
        out_v = out.rearrange("(p j) d -> p j d", j=NODE_J)
        table_v = table.rearrange("(p j) d -> p j d", j=NODE_J)
        FULL = (ALL_GROUPS - GROUPS)
        dst_v = dst[0:FULL * GROUP].rearrange("(r e) -> r e", e=GROUP)
        src_v = src[0:FULL * GROUP].rearrange("(r e) -> r e", e=GROUP)
        ea_v = ea4[0:FULL * GROUP, :].rearrange("(r e) c -> r (e c)", e=GROUP)
        dst_t = dst[LAST_START:EDGES].rearrange("(r e) -> r e", e=GROUP)
        src_t = src[LAST_START:EDGES].rearrange("(r e) -> r e", e=GROUP)
        ea_t = ea4[LAST_START:EDGES, :].rearrange("(r e) c -> r (e c)", e=GROUP)
        WHOLE = FULL // 128
        LEFT = FULL - 128 * WHOLE
        CUT, CUT_E = OVERLAP // GROUP, OVERLAP % GROUP
        acc_v = acc[:, 0:NODES].rearrange("q (p j) -> q p j", j=NODE_J)
        INDEX_LOADS = 3
        NODE_WEIGHT_LOADS = 8
        LOOP_WEIGHT_LOADS = 36
        OFFSETS_FROM = 8

        block = ctx.enter_context(nc.Block())

        @block.sync
        def _(sp):
            sp.wait_ge(s_zero_node, 2)
            sp.dma_start(wfeat[0:MUL, 0:MUL], W1_0e[:, 0:MUL]).then_inc(s_node_w, 16)
            sp.dma_start(wself_raw[0:MUL, 0:MUL], W1_0e[:, MUL:2 * MUL]).then_inc(s_node_w, 16)
            for i in range(3):
                cols = slice(MUL * (1 + i), MUL * (2 + i))
                sp.dma_start(wfeat[MUL + i:128:3, cols], W1_1o[:, 0:MUL]).then_inc(s_node_w, 16)
                sp.dma_start(wself_raw[MUL + i:128:3, cols], W1_1o[:, MUL:2 * MUL]).then_inc(s_node_w, 16)
            for n in range(PIECES):
                j = slice(n * PIECE, (n + 1) * PIECE)
                sp.dma_start(x_rows[:, j, :], x_v[:, j, :]).then_inc(s_x[n], 16)
                if n == 0:
                    sp.wait_ge(s_rows, 2)
                    for rows, whole, tail, s in ((dst_rows, dst_v, dst_t, s_dst), (src_rows, src_v, src_t, s_src)):
                        r = rows.bitcast(INT32)
                        sp.dma_start(r[:, 0:WHOLE, :], whole[0:128 * WHOLE, :].rearrange("(c p) e -> p c e", p=128))\
                            .then_inc(s, 16)
                        sp.dma_start(r[0:LEFT, WHOLE, :], whole[128 * WHOLE:, :]).then_inc(s, 16)
                        sp.dma_start(r[LEFT:LEFT + GROUPS, WHOLE, :], tail).then_inc(s, 16)
            for c in range(ROWS):
                if c == 2:
                    for n in range(PIECES):
                        sp.wait_ge(s_feats, (n + 1) * (PIECE // BATCH))
                        sp.dma_start(table_v[:, n * PIECE:(n + 1) * PIECE, :], feat_rows[:, n % 2]).then_inc(s_tab[n % 2], 16)
                if c >= 2:
                    sp.wait_ge(s_et, 2 * (c - 1))
                if c < WHOLE:
                    sp.dma_start(ea_rows[:, c % 2, :], ea_v[128 * c:128 * (c + 1), :]).then_inc(s_ea[c % 2], 16)
                else:
                    sp.wait_ge(s_eaz, 1)
                    sp.dma_start(ea_rows[0:LEFT, c % 2, :], ea_v[128 * c:, :]).then_inc(s_ea[c % 2], 16)
                    sp.dma_start(ea_rows[LEFT + CUT:LEFT + CUT + 1, c % 2, 4 * CUT_E:], ea_t[CUT:CUT + 1, 4 * CUT_E:])\
                        .then_inc(s_ea[c % 2], 16)
                    sp.dma_start(ea_rows[LEFT + CUT + 1:LEFT + GROUPS, c % 2, :], ea_t[CUT + 1:, :])\
                        .then_inc(s_ea[c % 2], 16)
                if c == 2:
                    sp.wait_ge(s_base13, 1)
                    sp.dma_start(base_dram, base13[:, :]).then_inc(s_bd, 16)
                if c == 4:
                    sp.wait_ge(s_bd, 16)
                    sp.dma_start(base_row[0:1, :], base_dram.rearrange("(a c) p -> a (c p)", a=1)).then_inc(s_br, 16)

            def e8_block(start):
                return ea8[bass.ds(start, BLOCK), :].rearrange("(p j) f -> p (j f)", p=128)

            sp.wait_ge(s_flag, 1)
            flag = sp.value_load(flag_i[0:1, 0:1], min_val=0, max_val=NODES)
            with sp.If(flag < WINDOW):
                for b in range(SLOTS):
                    if b == 0:
                        sp.wait_ge(s_xts, NODE_BATCHES)
                        sp.wait_ge(s_initp, NODE_BATCHES)
                    sp.dma_start(e8[:, b, :], e8_block(b * BLOCK)).then_inc(s_e8[b], 16)
                with sp.Fori(1, QUADS) as n:
                    for s in range(SLOTS):
                        sp.wait_ge(s_tr, n * SLOTS + (s - SLOTS + 1))
                        sp.dma_start(e8[:, s, :], e8_block((n * SLOTS + s) * BLOCK)).then_inc(s_e8[s], 16)
                for b in (BLOCKS - 2, BLOCKS - 1):
                    sp.wait_ge(s_tr, b - SLOTS + 1)
                    sp.dma_start(e8[:, b % SLOTS, :], e8_block(min(b * BLOCK, LAST_START))).then_inc(s_e8[b % SLOTS], 16)
            with sp.Else():
                sp.wait_ge(s_xts, NODE_BATCHES)
                sp.wait_ge(s_initp, NODE_BATCHES)
                with sp.Fori(0, BLOCKS - 1) as b:
                    sp.wait_ge(s_tr, b + 0)
                    sp.dma_start(e8[:, 0, :], e8_block(b * BLOCK)).then_inc(s_e8[0], 16)
                sp.wait_ge(s_tr, BLOCKS - 1)
                sp.dma_start(e8[:, 0, :], e8_block(LAST_START)).then_inc(s_e8[0], 16)
            for n in range(PIECES):
                j = slice(n * PIECE, (n + 1) * PIECE)
                sp.wait_ge(s_yr, (n + 1) * PIECE)
                sp.dma_start(out_v[:, j, :], x_rows[:, j, :]).then_inc(s_out, 16)
            sp.wait_ge(s_out, 16 * PIECES)

        @block.gpsimd
        def _(pool):
            pool.memset(wfeat[:, :], 0.0).then_inc(s_zero_node, 1)
            pool.memset(wself_raw, 0.0).then_inc(s_zero_node, 1)
            pool.memset(ident[:, :], 0.0).then_inc(s_ident0, 1)
            pool.wait_ge(s_ident0, 1)
            pool.affine_select(out=ident[:, :], in_=ident[:, :], compare_op=ALU.not_equal, fill=1.0, base=0,
                               pattern=[[-1, 128]], channel_multiplier=1).then_inc(s_ident, 1)
            pool.memset(dst_rows[:, ROWS - 1, :], 0.0).then_inc(s_rows, 1)
            pool.memset(src_rows[:, ROWS - 1, :], 0.0).then_inc(s_rows, 1)
            pool.iota(iota_i[:, :], pattern=[[1, WINDOW]], base=0, channel_multiplier=0).then_inc(s_iota, 1)
            pool.memset(eps_col[:, :], EPS).then_inc(s_iota, 1)
            pool.memset(w1bd[:, :, :], 0.0).then_inc(s_zero, 1)
            pool.memset(w2bd[:, :], 0.0).then_inc(s_zero, 1)
            pool.memset(wpbd[:, :], 0.0).then_inc(s_zero, 1)
            pool.memset(conv_stage[:, :, :], 0.0).then_inc(s_zero, 1)
            pool.wait_ge(s_zero, 4)
            for a in range(8):
                for e in range(2):
                    r = 16 * a + RADIAL * e
                    pool.dma_start(w1bd[r:r + RADIAL, a, HID * e:HID * (e + 1)], W_mlp1).then_inc(s_wts, 16)
            for e in range(2):
                h = slice(HID * e, HID * (e + 1))
                pool.dma_start(w2bd[h, h], W_mlp2).then_inc(s_wts, 16)
                for m in range(4):
                    pool.dma_start(wpbd[h, 128 * e + MUL * m:128 * e + MUL * (m + 1)], Wp[m]).then_inc(s_wts, 16)
            pool.dma_start(conv_stage[0:MUL, 0, 0:MUL], W2_0e[0:MUL, :]).then_inc(s_wts, 16)
            for i in range(3):
                m = slice(MUL * (1 + i), MUL * (2 + i))
                pool.dma_start(conv_stage[m, 0, m], W2_1o[MUL:2 * MUL, :]).then_inc(s_wts, 16)
                pool.dma_start(conv_stage[0:MUL, 1 + i, m], W2_1o[0:MUL, :]).then_inc(s_wts, 16)
                pool.dma_start(conv_stage[m, 1 + i, 0:MUL], W2_0e[MUL:2 * MUL, :]).then_inc(s_wts, 16)

            def gather(s, c):
                for t in range(CT * c, CT * (c + 1)):
                    pool.indirect_dma_start(out=gath[:, s, t, :], out_offset=None, in_=table[:, :],
                                            in_offset=bass.IndirectOffsetOnAxis(ap=idx[:, s, t:t + 1], axis=0))\
                        .then_inc(s_g[s][c], 16)

            def table_stored():
                pool.wait_ge(s_tab[0], 16 * -(-PIECES // 2))
                pool.wait_ge(s_tab[1], 16 * (PIECES // 2))

            table_stored()
            pool.wait_ge(s_flag, 1)
            flag = pool.value_load(flag_i[0:1, 0:1], min_val=0, max_val=NODES)
            with pool.If(flag < WINDOW):
                for b in range(SLOTS):
                    pool.wait_ge(s_idx, b + 1)
                    for c in range(CHUNKS):
                        gather(b, c)
                with pool.Fori(1, QUADS) as n:
                    for s in range(SLOTS):
                        pool.wait_ge(s_idx, n * SLOTS + (s + 1))
                        for c in range(CHUNKS):
                            pool.wait_ge(s_prod, n * (SLOTS * CHUNKS) + (CHUNKS * (s - SLOTS) + c + 1))
                            pool.sem_inc(s_round, 1)
                            gather(s, c)
                for b in (BLOCKS - 2, BLOCKS - 1):
                    pool.wait_ge(s_idx, b + 1)
                    for c in range(CHUNKS):
                        pool.wait_ge(s_prod, CHUNKS * (b - SLOTS) + c + 1)
                        gather(b % SLOTS, c)
            with pool.Else():
                with pool.Fori(0, BLOCKS) as b:
                    pool.wait_ge(s_idx, b + 1)
                    pool.sem_inc(s_round, 1)
                    for c in range(CHUNKS):
                        gather(0, c)

        @block.scalar
        def _(act):
            for n in range(NODE_BATCHES):
                act.wait_ge(s_xt, n + 1)
                if n >= 1:
                    act.wait_ge(s_initp, n)
                act.copy(xT[:, :, 0:NODE_P], bank[n % 2][:, 0:BATCH * NODE_P].rearrange("p (j n) -> p j n", j=BATCH))\
                    .then_inc(s_xts, 1)
                act.wait_ge(s_initp, n + 1)
                act.copy(acc_v[:, :, BATCH * n:BATCH * (n + 1)].rearrange("q p j -> q j p"),
                         bank[4 + n % 2][:, 0:BATCH * NODE_P].rearrange("q (j p) -> q j p", j=BATCH))\
                    .then_inc(s_inits, 1)

            def copy_indices(b, s):
                return act.copy(idx[:, s, :], src_all[:, bass.ds(b * TILES, TILES)])

            def copy_attributes():
                for c in range(ROWS):
                    r = rows_of(c)
                    dest = ea_all[:, 1024 * c:1024 * c + 8 * r].rearrange("q (g e k) -> q e k g", e=2, k=4)
                    for e in range(2):
                        act.wait_ge(s_et, 2 * c + e + 1)
                        act.copy(dest[:, e], bank[4 + e][:, :].rearrange("q (k g) -> q k g", k=4)[:, :, 0:r])\
                            .then_inc(s_ets, 1)

            def gelu1(b, h):
                act.wait_ge(s_h1p, b * 2 + (h + 1))
                act.activation(h1[:, h, :], hid_ps[h][:, :], ACT.Gelu_apprx_tanh,
                               scale=1.0 / math.sqrt(RADIAL)).then_inc(s_h1, 1)

            def gelu2(b, m, h):
                act.wait_ge(s_h2p, b * 2 + (h + 1))
                act.activation(h2[:, m % 2, :, 4 * h:4 * (h + 1)].rearrange("p e a -> p a e"),
                               hid_ps[h][:, :].rearrange("p (a e) -> p a e", a=4), ACT.Gelu_apprx_tanh,
                               scale=1.0 / math.sqrt(HID)).then_inc(s_h2, 1)

            def copy_e8T(b):
                act.wait_ge(s_tr, b + 1)
                act.copy(e8T[:, :], t_ps).then_inc(s_e8T, 1)

            def copy_sums(b):
                act.wait_ge(s_seg, b * CHUNKS + CHUNKS)
                act.copy(zsb[:, :], z_ps[:, :]).then_inc(s_zc, 1)

            def step(b, m, first=False, last=False):
                if not last:
                    copy_e8T(b + 1)
                    gelu1(b + 1, 0)
                    gelu1(b + 1, 1)
                if not first:
                    copy_sums(b - 1)
                if not last and not first:
                    copy_indices(b + (SLOTS - 1), (m + SLOTS - 1) % SLOTS).then_inc(s_idx, 1)
                if not last:
                    gelu2(b + 1, m + 1, 0)
                    gelu2(b + 1, m + 1, 1)

            act.wait_ge(s_flag, 1)
            flag = act.value_load(flag_i[0:1, 0:1], min_val=0, max_val=NODES)
            act.wait_ge(s_rts, 2)
            with act.If(flag < WINDOW):
                for b in range(SLOTS):
                    copy_indices(b, b).then_inc(s_idx, 1)
                copy_attributes()
                act.wait_ge(s_rts, 2 * ROWS)
                copy_e8T(0)
                gelu1(0, 0)
                gelu1(0, 1)
                gelu2(0, 0, 0)
                gelu2(0, 0, 1)
                step(0, 0, first=True)
                with act.Fori(0, QUADS) as n:
                    for s in range(1, SLOTS + 1):
                        step(n * SLOTS + s, s)
                step(BLOCKS - 1, BLOCKS - 1, last=True)
                copy_sums(BLOCKS - 1)
            with act.Else():
                copy_attributes()
                act.wait_ge(s_rts, 2 * ROWS)
                with act.Fori(0, BLOCKS) as b:
                    act.wait_ge(s_gblk, b + 0)
                    copy_indices(b, 0).then_inc(s_idx, 1)
                    copy_e8T(b)
                    gelu1(b, 0)
                    gelu1(b, 1)
                    gelu2(b, 0, 0)
                    gelu2(b, 0, 1)
                    for g in range(GROUPS):
                        act.wait_ge(s_gz, b * GROUPS + (g + 1))
                        for e in range(2):
                            last = act.copy(gen_z[:, e], bank[4 + e][:, :].rearrange("p (k n) -> p k n", k=4))
                        last.then_inc(s_gzc, 1)
            for n in range(NODE_BATCHES + 1):
                if n < NODE_BATCHES:
                    act.wait_ge(s_var, n + 1)
                    if n >= 4:
                        act.wait_ge(s_yr, BATCH * (n - 3))
                    act.activation(rstd[0:NODE_P, n % 4, :, 0], moments[0:NODE_P, n % 4, :, 1], ACT.Sqrt,
                                   bias=eps_col[0:NODE_P, :]).then_inc(s_std, 1)
                if n >= 1:
                    act.wait_ge(s_sc, n)
                    for j in range(BATCH):
                        act.activation(x_rows[:, BATCH * (n - 1) + j, :],
                                       bank[(n - 1) % 4][0:NODE_P, 128 * j:128 * (j + 1)], ACT.Identity,
                                       bias=rstd[0:NODE_P, (n - 1) % 4, j, 1:2],
                                       scale=rstd[0:NODE_P, (n - 1) % 4, j, 0:1]).then_inc(s_yr, 1)

        @block.tensor
        def _(pe):
            pe.wait_ge(s_ident, 1)
            for n in range(NODE_BATCHES):
                pe.wait_ge(s_x[n * BATCH // PIECE], 16)
                if n >= 2:
                    pe.wait_ge(s_xts, n - 1)
                for j in range(BATCH):
                    last = pe.transpose(bank[n % 2][:, NODE_P * j:NODE_P * (j + 1)], x_rows[:, BATCH * n + j, :],
                                        ident[0:NODE_P, 0:NODE_P])
                last.then_inc(s_xt, 1)
                if n == 0:
                    pe.wait_ge(s_wnode, 4)
                pe.wait_ge(s_xts, n + 1)
                if n >= 2:
                    pe.wait_ge(s_feats, n - 1)
                for j in range(BATCH):
                    last = pe.matmul(bank[2 + n % 2][0:NODE_P, 128 * j:128 * (j + 1)], xT[:, j, 0:NODE_P],
                                     wfeat[:, :], start=True, stop=True)
                last.then_inc(s_featp, 1)
                if n >= 2:
                    pe.wait_ge(s_inits, n - 1)
                pe.matmul(bank[4 + n % 2][:, 0:BATCH * NODE_P], winit[:, :], xT[:, :, 0:NODE_P],
                          start=True, stop=True).then_inc(s_initp, 1)
            pe.wait_ge(s_base, 1)
            pe.transpose(bank[7][0:ROWS, 0:128], base_f[:, :], ident[:, :])
            pe.transpose(bank[7][0:1, 128:256], relmax[:, ROWS:ROWS + 1], ident[:, :]).then_inc(s_small, 1)
            pe.wait_ge(s_src_f, 1)
            for c in range(ROWS):
                r = rows_of(c)
                if c >= 2:
                    pe.wait_ge(s_rts, 2 * (c - 1))
                for k, rows in enumerate((src_rows, dst_rows)):
                    for e in range(2):
                        at = 256 * k + 128 * e
                        last = pe.transpose(bank[c % 2][:, at:at + r], rows[0:r, c, e:256:2], ident[0:r, 0:r])
                last.then_inc(s_rt, 1)
            pe.wait_ge(s_inits, NODE_BATCHES)
            for c in range(ROWS):
                r = rows_of(c)
                pe.wait_ge(s_ea[c % 2], 16 * (c // 2 + 1) if c < WHOLE else 16 * (c // 2 + INDEX_LOADS))
                for e in range(2):
                    if c >= 1:
                        pe.wait_ge(s_ets, 2 * (c - 1) + e + 1)
                    for k in range(4):
                        last = pe.transpose(bank[4 + e][:, 128 * k:128 * k + r],
                                            ea_rows[0:r, c % 2, 4 * e + k:4 * GROUP:8], ident[0:r, 0:r])
                    last.then_inc(s_et, 1)
            pe.wait_ge(s_feats, NODE_BATCHES)
            pe.wait_ge(s_rts, 2 * ROWS)
            pe.wait_ge(s_ets, 2 * ROWS)
            pe.wait_ge(s_flag, 1)
            pe.wait_ge(s_wts, 16 * LOOP_WEIGHT_LOADS)
            pe.wait_ge(s_conv, 3)

            def transpose_e8(b, s, round_):
                pe.wait_ge(s_e8[s], round_ * 16 + 16)
                pe.wait_ge(s_h2, b * 2)
                pe.transpose(t_ps, e8[:, s, :], ident[:, :]).then_inc(s_tr, 1)

            def layer1(b, h, free=None):
                if h == 0:
                    pe.wait_ge(s_e8T, b + 1)
                if free is not None:
                    pe.wait_ge(s_h2, free)
                for a in range(4 * h, 4 * h + 4):
                    last = pe.matmul(hid_ps[h][:, 128 * (a % 4):128 * (a % 4 + 1)], w1bd[:, a, :], e8T[:, :],
                                     start=True, stop=True)
                last.then_inc(s_h1p, 1)

            def layer2(b, h):
                pe.wait_ge(s_h1, b * 2 + (h + 1))
                pe.matmul(hid_ps[h][:, :], w2bd[:, :], h1[:, h, :], start=True, stop=True).then_inc(s_h2p, 1)

            def radial(b, m, c, first=False):
                if c == 0:
                    pe.wait_ge(s_h2, b * 2 + 2)
                if not first:
                    pe.wait_ge(s_prod, b * CHUNKS + (c + 1 - CHUNKS))
                for r in range(2):
                    g = 2 * c + r
                    last = pe.matmul(wgt_ps[c][:, 256 * r:256 * (r + 1)],
                                     h2[:, m % 2, 16 * g:16 * (g + 1), :].rearrange("p e a -> p (e a)"), wpbd[:, :],
                                     start=True, stop=True)
                last.then_inc(s_w, 1)

            def segment_sum(b, m, c, first=False):
                if c == 0:
                    pe.wait_ge(s_sel, b + 1)
                    if not first:
                        pe.wait_ge(s_zc, b + 0)
                pe.wait_ge(s_prod, b * CHUNKS + (c + 1))
                for r in range(2):
                    g = 2 * c + r
                    for half, at, n in ((0, 0, 1), (1, WINDOW, 3)):
                        o = 4 * WINDOW * g + at
                        for e in range(2):
                            last = pe.matmul(z_ps[:, o:o + n * WINDOW],
                                             prod[:, c, 2 * r + e, 128 * half:128 * (half + 1)],
                                             sel[:, m % 2, 2 * g + e, half:half + n, :], start=(e == 0), stop=(e == 1))
                last.then_inc(s_seg, 1)

            def convolve(b):
                pe.wait_ge(s_zc, b + 1)
                pe.wait_ge(s_add, b * GROUPS)
                for k in range(4):
                    last = pe.matmul(y_ps, conv[:, k, :],
                                     zsb[:, :].rearrange("p (g k w) -> p g k w", g=GROUPS, k=4)[:, :, k, :],
                                     start=(k == 0), stop=(k == 3))
                last.then_inc(s_y, 1)

            def step(b, m, round_, first=False, last=False):
                for c in range(CHUNKS):
                    if c == 0 and not last:
                        transpose_e8(b + 1, (m + 1) % SLOTS, round_)
                    radial(b, m, c, first)
                    if not last:
                        if c < 2:
                            layer1(b + 1, c, b * 2 + (c + 1))
                        else:
                            layer2(b + 1, c - 2)
                    if c >= 2:
                        segment_sum(b, m, c - 2, first)
                    elif not first:
                        segment_sum(b - 1, m - 1, c + 2)
                    if c == 2 and not first:
                        convolve(b - 1)

            flag = pe.value_load(flag_i[0:1, 0:1], min_val=0, max_val=NODES)
            with pe.If(flag < WINDOW):
                transpose_e8(0, 0, 0)
                layer1(0, 0)
                layer1(0, 1)
                layer2(0, 0)
                layer2(0, 1)
                step(0, 0, 0, first=True)
                with pe.Fori(0, QUADS) as n:
                    for s in range(1, SLOTS + 1):
                        step(n * SLOTS + s, s, n + (s + 1) // SLOTS)
                step(BLOCKS - 1, BLOCKS - 1, 0, last=True)
                segment_sum(BLOCKS - 1, BLOCKS - 1, 2)
                segment_sum(BLOCKS - 1, BLOCKS - 1, 3)
                convolve(BLOCKS - 1)
                pe.wait_ge(s_add, BLOCKS * GROUPS)
            with pe.Else():
                with pe.Fori(0, BLOCKS) as b:
                    transpose_e8(b, 0, b)
                    layer1(b, 0)
                    layer1(b, 1)
                    layer2(b, 0)
                    layer2(b, 1)
                    pe.wait_ge(s_h2, b * 2 + 2)
                    for g in range(GROUPS):
                        pe.wait_ge(s_gprod, b * GROUPS + g)
                        pe.matmul(wgt_ps[0][:, 0:256], h2[:, 0, 16 * g:16 * (g + 1), :].rearrange("p e a -> p (e a)"),
                                  wpbd[:, :], start=True, stop=True).then_inc(s_gw, 1)
                        pe.wait_ge(s_gdiag, b * GROUPS + (g + 1))
                        pe.wait_ge(s_gprod, b * GROUPS + (g + 1))
                        for e in range(2):
                            for half, n in ((0, 1), (1, 3)):
                                last = pe.matmul(bank[4 + e][:, 128 * half:128 * (half + n)],
                                                 prod[:, 0, e, 128 * half:128 * (half + 1)],
                                                 diag[:, e, half:half + n, :], start=True, stop=True)
                        last.then_inc(s_gz, 1)
                        pe.wait_ge(s_gzc, b * GROUPS + (g + 1))
                        for k in range(4):
                            last = pe.matmul(z_ps[:, 0:256], conv[:, k, :], gen_z[:, :, k, :],
                                             start=(k == 0), stop=(k == 3))
                        last.then_inc(s_gy, 1)
                    pe.wait_ge(s_gblk, b + 1)
            for n in range(NODE_BATCHES):
                if n >= 4:
                    pe.wait_ge(s_yr, BATCH * (n - 3))
                for j in range(BATCH):
                    last = pe.transpose(bank[n % 4][0:NODE_P, 128 * j:128 * (j + 1)], acc_v[:, :, BATCH * n + j],
                                        ident[:, :])
                last.then_inc(s_ft, 1)

        @block.vector
        def _(dve):
            links = [0]

            def link(instruction):
                links[0] += 1
                instruction.then_inc(s_prep, 1)
                dve.wait_ge(s_prep, links[0])

            dve.wait_ge(s_node_w, 16 * NODE_WEIGHT_LOADS)
            dve.wait_ge(s_ident, 1)
            dve.tensor_scalar(wfeat[:, :], wfeat[:, :], FEAT_SCALE, None, ALU.mult).then_inc(s_wnode, 1)
            dve.scalar_tensor_tensor(winit[:, 0:MUL], wself_raw[:, 0:MUL], SELF_SCALE, ident[:, 0:MUL],
                                     ALU.mult, ALU.add).then_inc(s_wnode, 1)
            by_unit = lambda ap: ap.rearrange("p (w i) -> p i w", i=3)
            dve.scalar_tensor_tensor(by_unit(winit[:, MUL:128]), wself_raw[:, MUL:128].rearrange("p (i w) -> p i w", i=3),
                                     SELF_SCALE, by_unit(ident[:, MUL:128]), ALU.mult, ALU.add).then_inc(s_wnode, 1)
            dve.wait_ge(s_iota, 2)
            dve.tensor_copy(iota_w[:, :], iota_i[:, :]).then_inc(s_wnode, 1)
            dve.memset(src_all[:, ALL_GROUPS * 2:], 0).then_inc(s_wnode, 1)
            dve.memset(acc[:, NODES:], 0.0).then_inc(s_wnode, 1)

            dst_i, src_i = dst_rows.bitcast(INT32), src_rows.bitcast(INT32)

            def offsets(c):
                link(dve.tensor_reduce(base_f[:, c:c + 1], dst_i[:, c, :], AXIS_X, ALU.min))
                link(dve.tensor_scalar(dst_rows[:, c, :], dst_i[:, c, :], base_f[:, c:c + 1], None, ALU.subtract))
                link(dve.tensor_reduce(relmax[:, c:c + 1], dst_rows[:, c, :], AXIS_X, ALU.max))

            per_piece = PIECE // BATCH
            for n in range(NODE_BATCHES):
                piece = n // per_piece
                dve.wait_ge(s_featp, n + 1)
                if n % per_piece == 0 and piece >= 2:
                    dve.wait_ge(s_tab[piece % 2], 16 * (piece // 2))
                j = BATCH * (n % per_piece)
                dve.tensor_copy(feat_rows[:, piece % 2, j:j + BATCH, :],
                                bank[2 + n % 2][0:NODE_P, :].rearrange("p (j f) -> p j f", j=BATCH)).then_inc(s_feats, 1)
                if OFFSETS_FROM <= n < OFFSETS_FROM + ROWS:
                    if n == OFFSETS_FROM:
                        dve.wait_ge(s_dst, 16 * INDEX_LOADS)
                    offsets(n - OFFSETS_FROM)
            dve.tensor_reduce(relmax[:, ROWS:ROWS + 1], relmax[:, 0:ROWS], AXIS_X, ALU.max).then_inc(s_base, 1)
            dve.wait_ge(s_src, 16 * INDEX_LOADS)
            dve.tensor_copy(src_rows[:, :, :], src_i[:, :, :]).then_inc(s_src_f, 1)
            dve.wait_ge(s_small, 1)
            dve.tensor_reduce(flag_i[0:1, 0:1], bank[7][0:1, 128:256], AXIS_X, ALU.max).then_inc(s_flag, 1)
            dve.tensor_copy(base13[:, :], bank[7][0:ROWS, 0:128]).then_inc(s_base13, 1)
            for c in range(ROWS):
                r = rows_of(c)
                dve.wait_ge(s_rt, c + 1)
                ps = bank[c % 2][:, :].rearrange("q (k e g) -> q k e g", k=2, e=2)
                for k, every in enumerate((src_all, rel_all)):
                    dve.tensor_copy(every[:, 256 * c:256 * c + 2 * r].rearrange("q (g e) -> q e g", e=2),
                                    ps[:, k, :, 0:r]).then_inc(s_rts, 1)
            dve.wait_ge(s_wts, 16 * LOOP_WEIGHT_LOADS)
            dve.tensor_scalar(conv[:, :, MUL:128].rearrange("p k (w i) -> p k i w", i=3),
                              conv_stage[:, :, MUL:128].rearrange("p k (i w) -> p k i w", i=3),
                              CONV_SCALE, None, ALU.mult).then_inc(s_conv, 1)
            dve.tensor_scalar(conv[:, 0, 0:MUL], conv_stage[:, 0, 0:MUL], CONV_SCALE, None, ALU.mult).then_inc(s_conv, 1)
            dve.tensor_scalar(conv[:, 1:4, 0:MUL], conv_stage[:, 1:4, 0:MUL], CONV_SCALE * INV_SQRT3, None,
                              ALU.mult).then_inc(s_conv, 1)
            dve.wait_ge(s_et, 2 * (ROWS - 2))
            dve.memset(ea_rows[:, (ROWS - 1) % 2, :], 0.0).then_inc(s_eaz, 1)
            dve.wait_ge(s_ets, 2 * ROWS)
            dve.wait_ge(s_inits, NODE_BATCHES)

            def select(b, m, free=None):
                ts_ = bass.ds(b * TILES, TILES)
                if free is not None:
                    dve.wait_ge(s_seg, free)
                dve.wait_ge(s_sel, b + 0)
                dve.tensor_tensor(sel01[:, :, :], rel_all[:, ts_].unsqueeze(2).to_broadcast([128, TILES, WINDOW]),
                                  iota_w[:, :].unsqueeze(1).to_broadcast([128, TILES, WINDOW]),
                                  ALU.is_equal).then_inc(s_sel0, 1)
                dve.wait_ge(s_sel0, b + 1)
                attr = ea_all[:, bass.ds(b * (TILES * 4), TILES * 4)].rearrange("q (t k) -> q t k", k=4)
                dve.tensor_tensor(sel[:, m % 2], sel01[:, :, :].unsqueeze(2).to_broadcast([128, TILES, 4, WINDOW]),
                                  attr.unsqueeze(3).to_broadcast([128, TILES, 4, WINDOW]), ALU.mult).then_inc(s_sel, 1)

            def multiply(weights, rows, to, n):
                w = weights.rearrange("q (t h a u) -> q t h a u", t=n, h=2, a=2)
                f = rows.rearrange("q t (s u) -> q t s u", s=4)
                o = to.rearrange("q t (h s u) -> q t h s u", h=2, s=4)
                dve.tensor_tensor(o[:, :, :, 0, :], w[:, :, :, 0, :],
                                  f[:, :, 0, :].unsqueeze(2).to_broadcast([128, n, 2, MUL]), ALU.mult)
                for h in range(2):
                    last = dve.tensor_tensor(o[:, :, h, 1:4, :],
                                             w[:, :, h, 1, :].unsqueeze(2).to_broadcast([128, n, 3, MUL]),
                                             f[:, :, 1:4, :], ALU.mult)
                return last

            def products(b, m, c, round_, first=False):
                dve.wait_ge(s_w, b * CHUNKS + (c + 1))
                dve.wait_ge(s_g[m % SLOTS][c], round_ * (16 * CT) + 16 * CT)
                if not first:
                    dve.wait_ge(s_seg, b * CHUNKS + (c + 1 - CHUNKS))
                multiply(wgt_ps[c][:, :], gath[:, m % SLOTS, CT * c:CT * (c + 1), :], prod[:, c], CT).then_inc(s_prod, 1)

            def add_windows(b):
                _, base = nc.values_load_multi_w_load_instructions(
                    base_row[0:1, bass.ds(b * GROUPS, GROUPS)], engines=(mybir.EngineType.DVE,),
                    min_val=0, max_val=NODES - 1)
                dve.wait_ge(s_y, b + 1)
                for g in range(GROUPS):
                    dve.wait_ge(s_add, b * GROUPS + g)
                    at = bass.ds(base[g], WINDOW)
                    dve.tensor_tensor(acc[:, at], acc[:, at], y_ps[:, WINDOW * g:WINDOW * (g + 1)], ALU.add)\
                        .then_inc(s_add, 1)

            def step(b, m, round_, first=False, last=False):
                if not last:
                    select(b + 1, m + 1, None if first else b * CHUNKS)
                for c in range(CHUNKS):
                    products(b, m, c, round_, first)
                if not first:
                    add_windows(b - 1)

            flag = dve.value_load(flag_i[0:1, 0:1], min_val=0, max_val=NODES)
            dve.wait_ge(s_br, 16)
            with dve.If(flag < WINDOW):
                select(0, 0)
                step(0, 0, 0, first=True)
                with dve.Fori(0, QUADS) as n:
                    for s in range(1, SLOTS + 1):
                        step(n * SLOTS + s, s, n + s // SLOTS)
                step(BLOCKS - 1, BLOCKS - 1, (BLOCKS - 1) // SLOTS, last=True)
                add_windows(BLOCKS - 1)
            with dve.Else():
                def general_block(b, start):
                    for c in range(CHUNKS):
                        dve.wait_ge(s_g[0][c], b * (16 * CT) + 16 * CT)
                    for g in range(GROUPS):
                        for e in range(2):
                            attr = ea_all[:, bass.ds(b * (TILES * 4) + 4 * (2 * g + e), 4)]
                            last = dve.tensor_tensor(diag[:, e], ident[:, :].unsqueeze(1).to_broadcast([128, 4, 128]),
                                                     attr.unsqueeze(2).to_broadcast([128, 4, 128]), ALU.mult)
                        last.then_inc(s_gdiag, 1)
                        dve.wait_ge(s_gw, b * GROUPS + (g + 1))
                        multiply(wgt_ps[0][:, 0:256], gath[:, 0, 2 * g:2 * g + 2, :], prod[:, 0, 0:2], 2)\
                            .then_inc(s_gprod, 1)
                        columns = z_ps[:, 0:256].rearrange("f (e n) -> f n e", e=2)
                        with dve.Fori(0, GROUP // 4) as n:
                            _, node = nc.values_load_multi_w_load_instructions(
                                dst[bass.ds(start + GROUP * g + n * 4, 4)].rearrange("(a n) -> a n", a=1),
                                engines=(mybir.EngineType.DVE,), min_val=0, max_val=NODES - 1)
                            dve.wait_ge(s_gy, b * GROUPS + (g + 1))
                            for k in range(4):
                                dve.wait_ge(s_add, b * BLOCK + n * 4 + (GROUP * g + k))
                                at = bass.ds(node[k], 1)
                                dve.tensor_tensor(acc[:, at], acc[:, at], columns[:, bass.ds(n * 2 + k // 2, 1), k % 2],
                                                  ALU.add).then_inc(s_add, 1)
                    dve.wait_ge(s_add, b * BLOCK + BLOCK)
                    dve.memset(flag_i[0:1, 1:2], 0).then_inc(s_gblk, 1)

                with dve.Fori(0, BLOCKS - 1) as b:
                    general_block(b, b * BLOCK)
                general_block(BLOCKS - 1, LAST_START)

            def moments_of(n):
                dve.wait_ge(s_ft, n + 1)
                for j in range(BATCH):
                    last = dve.bn_stats(stats[0:NODE_P, n % 4, j, :], bank[n % 4][0:NODE_P, 128 * j:128 * (j + 1)])
                link(last)
                for j in range(BATCH):
                    last = dve.bn_aggr(moments[0:NODE_P, n % 4, j, :], stats[0:NODE_P, n % 4, j, :])
                last.then_inc(s_var, 1)

            def scales_of(n):
                dve.wait_ge(s_std, n + 1)
                r = rstd[0:NODE_P, n % 4]
                link(dve.reciprocal(r[:, :, 0], r[:, :, 0]))
                dve.scalar_tensor_tensor(r[:, :, 1], moments[0:NODE_P, n % 4, :, 0], -1.0, r[:, :, 0],
                                         ALU.mult, ALU.mult).then_inc(s_sc, 1)

            for n in range(NODE_BATCHES + 1):
                if n < NODE_BATCHES:
                    moments_of(n)
                if n >= 1:
                    scales_of(n - 1)
    return nc


_INS = ['x', 'src', 'dst', 'edge_attr_4', 'edge_attr_8', 'L0_gnn_W1_0e', 'L0_gnn_W1_1o', 'L0_gnn_W_mlp1',
        'L0_gnn_W_mlp2', 'L0_gnn_Wp_00', 'L0_gnn_Wp_01', 'L0_gnn_Wp_10', 'L0_gnn_Wp_11', 'L0_gnn_W2_0e', 'L0_gnn_W2_1o']


def kernel(**inputs):
    import numpy as np
    import concourse.bacc as bacc
    from concourse.bass_utils import run_bass_kernel_spmd

    nc = bacc.Bacc("TRN2", target_bir_lowering=False, num_devices=1)
    arrays, aps = {}, {}
    for name in _INS:
        a = np.ascontiguousarray(inputs[name])
        arrays[f"in_{name}"] = a
        aps[name] = nc.dram_tensor(f"in_{name}", a.shape, mybir.dt.from_np(a.dtype), kind="ExternalInput").ap()
    out = nc.dram_tensor("out_0", (NODES, FEAT), FP32, kind="ExternalOutput").ap()
    w = {name.removeprefix("L0_gnn_"): aps[name] for name in _INS[5:]}
    build_program(nc, aps['x'], aps['src'], aps['dst'], aps['edge_attr_4'], aps['edge_attr_8'], w['W1_0e'], w['W1_1o'],
                  w['W_mlp1'], w['W_mlp2'], [w['Wp_00'], w['Wp_10'], w['Wp_01'], w['Wp_11']], w['W2_0e'], w['W2_1o'], out)
    r = run_bass_kernel_spmd(nc, [arrays], core_ids=[0])
    return r.results[0]["out_0"]
```

```python
import math

import concourse.bass as bass
from concourse import mybir
from contextlib import ExitStack

FP32 = mybir.dt.float32
INT32 = mybir.dt.int32
INT16 = mybir.dt.int16
BF16 = mybir.dt.bfloat16
ALU = mybir.AluOpType
ACT = mybir.ActivationFunctionType
AXIS_X = mybir.AxisListType.X

NODES, FEAT, EDGES = 12500, 128, 412500
MUL, RADIAL, HID = 32, 8, 64
NODE_P = 125
NODE_J = NODES // NODE_P
BATCH = 4
NODE_BATCHES = NODE_J // BATCH
PIECE = 20
PIECES = NODE_J // PIECE
LOADS = (0, 4, 20, 40, 60, 80, 100)
STORES = (0, 20, 40, 60, 80, 92, 100)
NORM = 8
NORM_BATCHES = -(-NODE_J // NORM)
GROUP = 256
BLOCK = 2048
GROUPS = BLOCK // GROUP
TILES = BLOCK // 128
CHUNKS = 4
CT = TILES // CHUNKS
BLOCKS = -(-EDGES // BLOCK)
LAST_START = EDGES - BLOCK
OVERLAP = BLOCKS * BLOCK - EDGES
ALL_GROUPS = BLOCKS * GROUPS
ROWS = -(-ALL_GROUPS // 128)
WINDOW = 16
SLOTS = 4
QUADS = (BLOCKS - 2) // SLOTS
assert BLOCKS == 2 + SLOTS * QUADS

MIX = math.pi / 8.0
SELF_SCALE = math.cos(MIX) / math.sqrt(MUL)
FEAT_SCALE = 1.0 / math.sqrt(MUL)
CONV_SCALE = math.sin(MIX) / math.sqrt(2.0) / math.sqrt(32.0) / math.sqrt(2.0 * MUL)
INV_SQRT3 = 1.0 / math.sqrt(3.0)
EPS = 1e-05


def rows_of(c):
    return min(128, ALL_GROUPS - 128 * c)


def build_program(nc, x, src, dst, ea4, ea8, W1_0e, W1_1o, W_mlp1, W_mlp2, Wp, W2_0e, W2_1o, out):
    ctx = ExitStack()
    with ctx:
        def sb(name, shape, dt=FP32):
            return ctx.enter_context(nc.sbuf_tensor(name, shape, dt))

        def sem(name):
            return ctx.enter_context(nc.semaphore(name))

        table = nc.dram_tensor("feature_table", [NODES, FEAT], FP32, kind="Internal").ap()
        base_dram = nc.dram_tensor("group_bases", [ROWS, 128], INT32, kind="Internal").ap()

        acc = sb("acc", [128, NODES + WINDOW])
        ea_all = sb("ea_all", [128, ALL_GROUPS * 2 * 4])
        rel_all = sb("rel_all", [128, ALL_GROUPS * 2], BF16)
        src_all = sb("src_all", [128, (BLOCKS + 2) * TILES], INT16)
        gath = sb("gath", [128, SLOTS, TILES, FEAT])
        idx = sb("idx", [128, SLOTS, TILES], INT32)
        e8 = sb("e8", [128, SLOTS, 128])
        e8T = sb("e8T", [128, 128])
        zsb = sb("zsb", [128, GROUPS * 4 * WINDOW])
        ident = sb("ident", [128, 128])
        iota_i = sb("iota_i", [128, WINDOW], INT32)
        iota_w = sb("iota_w", [128, WINDOW], BF16)
        w1bd = sb("w1bd", [128, 8, 128])
        w2bd = sb("w2bd", [128, 128])
        wpbd = sb("wpbd", [128, 2 * 128])
        wfeat = sb("wfeat", [128, 128])
        winit = sb("winit", [128, 128])
        conv = sb("conv", [128, 4, 128])
        base_f = sb("base_f", [128, ROWS])
        relmax = sb("relmax", [128, ROWS + 1])
        base13 = sb("base13", [ROWS, 128], INT32)
        base_row = sb("base_row", [1, ROWS * 128], INT32)
        flag_i = sb("flag_i", [1, 8], INT32)
        stats = sb("stats", [128, 4, NORM, 6])
        moments = sb("moments", [128, 4, NORM, 2])
        rstd = sb("rstd", [128, 4, NORM, 2])
        eps_col = sb("eps_col", [128, 1])

        work = sb("work", [128, 9216])
        prod = work[:, 0:4096].rearrange("p (c t f) -> p c t f", c=CHUNKS, t=CT)
        sel = work[:, 4096:6144].rearrange("p (b t k w) -> p b t k w", b=2, t=TILES, k=4)
        h1 = work[:, 6144:7168].rearrange("p (h n) -> p h n", h=2)
        h2 = work[:, 7168:9216].rearrange("p (b e a) -> p b e a", b=2, a=8)
        dst_rows = work[:, 0:ROWS * 256].rearrange("p (c e) -> p c e", c=ROWS)
        src_rows = work[:, ROWS * 256:2 * ROWS * 256].rearrange("p (c e) -> p c e", c=ROWS)
        ea_rows = work[:, 2 * ROWS * 256:2 * ROWS * 256 + 2048].rearrange("p (b e) -> p b e", b=2)
        assert 2 * ROWS * 256 + 2048 <= 9216
        wself_raw = zsb[:, 0:128]
        x_rows = ea_all[0:NODE_P, 0:NODE_J * FEAT].rearrange("p (j d) -> p j d", d=FEAT)
        feat_rows = gath[0:NODE_P, :, :, :].rearrange("p s t f -> p (s t) f")[:, 0:2 * PIECE, :]\
            .rearrange("p (b j) f -> p b j f", b=2)
        sel01 = sb("sel01", [128, TILES, WINDOW])
        conv_stage = sb("conv_stage", [128, 4, 128])
        diag = work[:, 4096:5120].rearrange("p (t k n) -> p t k n", t=2, k=4)
        gen_z = work[:, 3072:4096].rearrange("p (t k n) -> p t k n", t=2, k=4)

        bank = [ctx.enter_context(nc.psum_tensor(f"bank{i}", [128, 512], FP32)) for i in range(8)]
        hid_ps = [bank[0], bank[1]]
        wgt_ps = [bank[2], bank[3], bank[4], bank[5]]
        z_ps = bank[6]
        t_ps = bank[0][:, 0:128]
        y_ps = bank[7][:, 0:128]

        s_node_w = sem("node_weights_in")
        s_x = [sem(f"x_in{i}") for i in range(len(LOADS) - 1)]
        s_rows = sem("index_rows_zeroed")
        s_dst = sem("dst_in")
        s_src = sem("src_in")
        s_ea = [sem(f"ea_in{i}") for i in range(2)]
        s_eaz = sem("ea_tail_zeroed")
        s_zero = sem("weights_zeroed")
        s_zero_node = sem("node_weights_zeroed")
        s_wts = sem("loop_weights_in")
        s_ident0 = sem("ident_zeroed")
        s_ident = sem("ident_ready")
        s_iota = sem("iota_ready")
        s_prep = sem("vector_chain")
        s_wnode = sem("node_weights_ready")
        s_xt = sem("x_transposed")
        s_xts = sem("x_transposed_copied")
        s_featp = sem("features_done")
        s_feats = sem("features_copied")
        s_initp = sem("init_done")
        s_inits = sem("init_copied")
        s_tab = [sem(f"table_stored{i}") for i in range(2)]
        s_src_f = sem("src_as_float")
        s_base = sem("bases_ready")
        s_small = sem("small_transposes_done")
        s_base13 = sem("bases_transposed")
        s_bd = sem("bases_in_dram")
        s_br = sem("bases_in_row")
        s_flag = sem("flag_ready")
        s_rt = sem("index_transposes_done")
        s_rts = sem("index_transposes_copied")
        s_et = sem("ea_transposes_done")
        s_ets = sem("ea_transposes_copied")
        s_conv = sem("conv_weights_ready")
        s_e8 = [sem(f"e8_in{i}") for i in range(SLOTS)]
        s_tr = sem("e8_transposed")
        s_e8T = sem("e8_transposed_copied")
        s_h1p = [sem(f"layer1_done{h}") for h in range(2)]
        s_h1 = [sem(f"gelu1_done{h}") for h in range(2)]
        s_h2p = [sem(f"layer2_done{h}") for h in range(2)]
        s_h2 = [sem(f"gelu2_done{h}") for h in range(2)]
        s_w = [sem(f"radial_weights_done{c}") for c in range(CHUNKS)]
        s_idx = sem("indices_ready")
        s_g = [[sem(f"gathered{s}_{c}") for c in range(CHUNKS)] for s in range(SLOTS)]
        s_round = sem("gather_slot_seen_free")
        s_sel0 = sem("onehot_ready")
        s_sel = sem("selection_ready")
        s_prod = [sem(f"products_ready{c}") for c in range(CHUNKS)]
        s_seg = [sem(f"segments_summed{c}") for c in range(CHUNKS)]
        s_zc = sem("sums_copied")
        s_y = sem("conv_done")
        s_add = [sem(f"window_added{g}") for g in range(GROUPS)]
        s_gadd = sem("general_edge_added")
        s_gz = sem("general_sums_done")
        s_gzc = sem("general_sums_copied")
        s_gprod = sem("general_products_ready")
        s_gdiag = sem("general_diagonals_ready")
        s_gw = sem("general_weights_done")
        s_gy = sem("general_conv_done")
        s_gblk = sem("general_block_added")
        s_ft = sem("rows_transposed")
        s_var = sem("variance_ready")
        s_std = sem("std_ready")
        s_sc = sem("scale_ready")
        s_yr = sem("rows_normalised")
        s_out = sem("out_stored")

        x_v = x.rearrange("(p j) d -> p j d", j=NODE_J)
        out_v = out.rearrange("(p j) d -> p j d", j=NODE_J)
        table_v = table.rearrange("(p j) d -> p j d", j=NODE_J)
        FULL = (ALL_GROUPS - GROUPS)
        dst_v = dst[0:FULL * GROUP].rearrange("(r e) -> r e", e=GROUP)
        src_v = src[0:FULL * GROUP].rearrange("(r e) -> r e", e=GROUP)
        ea_v = ea4[0:FULL * GROUP, :].rearrange("(r e) c -> r (e c)", e=GROUP)
        dst_t = dst[LAST_START:EDGES].rearrange("(r e) -> r e", e=GROUP)
        src_t = src[LAST_START:EDGES].rearrange("(r e) -> r e", e=GROUP)
        ea_t = ea4[LAST_START:EDGES, :].rearrange("(r e) c -> r (e c)", e=GROUP)
        WHOLE = FULL // 128
        LEFT = FULL - 128 * WHOLE
        CUT, CUT_E = OVERLAP // GROUP, OVERLAP % GROUP
        acc_v = acc[:, 0:NODES].rearrange("q (p j) -> q p j", j=NODE_J)
        INDEX_LOADS = 3
        NODE_WEIGHT_LOADS = 8
        LOOP_WEIGHT_LOADS = 36
        OFFSETS_FROM = 6
        INIT = NODES // NODE_BATCHES
        assert NODE_BATCHES == 2 * ROWS - 1

        def norm_tiles(n):
            return min(NORM, NODE_J - NORM * n)

        def norm_ps(n, j):
            return bank[2 * (n % 4) + j // 4][0:NODE_P, 128 * (j % 4):128 * (j % 4 + 1)]

        block = ctx.enter_context(nc.Block())

        @block.sync
        def _(sp):
            for n in range(len(LOADS) - 1):
                j = slice(LOADS[n], LOADS[n + 1])
                sp.dma_start(x_rows[:, j, :], x_v[:, j, :]).then_inc(s_x[n], 16)
                if n == 2:
                    sp.wait_ge(s_rows, 2)
                    for rows, whole, tail, s in ((dst_rows, dst_v, dst_t, s_dst), (src_rows, src_v, src_t, s_src)):
                        r = rows.bitcast(INT32)
                        sp.dma_start(r[:, 0:WHOLE, :], whole[0:128 * WHOLE, :].rearrange("(c p) e -> p c e", p=128))\
                            .then_inc(s, 16)
                        sp.dma_start(r[0:LEFT, WHOLE, :], whole[128 * WHOLE:, :]).then_inc(s, 16)
                        sp.dma_start(r[LEFT:LEFT + GROUPS, WHOLE, :], tail).then_inc(s, 16)
            for c in range(ROWS):
                if c == 2:
                    for n in range(PIECES):
                        sp.wait_ge(s_feats, (n + 1) * (PIECE // BATCH))
                        sp.dma_start(table_v[:, n * PIECE:(n + 1) * PIECE, :], feat_rows[:, n % 2]).then_inc(s_tab[n % 2], 16)
                if c >= 2:
                    sp.wait_ge(s_et, 2 * (c - 1))
                if c < WHOLE:
                    sp.dma_start(ea_rows[:, c % 2, :], ea_v[128 * c:128 * (c + 1), :]).then_inc(s_ea[c % 2], 16)
                else:
                    sp.wait_ge(s_eaz, 1)
                    sp.dma_start(ea_rows[0:LEFT, c % 2, :], ea_v[128 * c:, :]).then_inc(s_ea[c % 2], 16)
                    sp.dma_start(ea_rows[LEFT + CUT:LEFT + CUT + 1, c % 2, 4 * CUT_E:], ea_t[CUT:CUT + 1, 4 * CUT_E:])\
                        .then_inc(s_ea[c % 2], 16)
                    sp.dma_start(ea_rows[LEFT + CUT + 1:LEFT + GROUPS, c % 2, :], ea_t[CUT + 1:, :])\
                        .then_inc(s_ea[c % 2], 16)
                if c == 2:
                    sp.wait_ge(s_base13, 1)
                    sp.dma_start(base_dram, base13[:, :]).then_inc(s_bd, 16)
                if c == 4:
                    sp.wait_ge(s_bd, 16)
                    sp.dma_start(base_row[0:1, :], base_dram.rearrange("(a c) p -> a (c p)", a=1)).then_inc(s_br, 16)

            def e8_block(start):
                return ea8[bass.ds(start, BLOCK), :].rearrange("(p j) f -> p (j f)", p=128)

            sp.wait_ge(s_flag, 1)
            flag = sp.value_load(flag_i[0:1, 0:1], min_val=0, max_val=NODES)
            with sp.If(flag < WINDOW):
                for b in range(SLOTS):
                    sp.dma_start(e8[:, b, :], e8_block(b * BLOCK)).then_inc(s_e8[b], 16)
                with sp.Fori(1, QUADS) as n:
                    for s in range(SLOTS):
                        sp.wait_ge(s_tr, n * SLOTS + (s - SLOTS + 1))
                        sp.dma_start(e8[:, s, :], e8_block((n * SLOTS + s) * BLOCK)).then_inc(s_e8[s], 16)
                for b in (BLOCKS - 2, BLOCKS - 1):
                    sp.wait_ge(s_tr, b - SLOTS + 1)
                    sp.dma_start(e8[:, b % SLOTS, :], e8_block(min(b * BLOCK, LAST_START))).then_inc(s_e8[b % SLOTS], 16)
            with sp.Else():
                with sp.Fori(0, BLOCKS - 1) as b:
                    sp.wait_ge(s_tr, b + 0)
                    sp.dma_start(e8[:, 0, :], e8_block(b * BLOCK)).then_inc(s_e8[0], 16)
                sp.wait_ge(s_tr, BLOCKS - 1)
                sp.dma_start(e8[:, 0, :], e8_block(LAST_START)).then_inc(s_e8[0], 16)
            for n in range(len(STORES) - 1):
                j = slice(STORES[n], STORES[n + 1])
                sp.wait_ge(s_yr, STORES[n + 1])
                sp.dma_start(out_v[:, j, :], x_rows[:, j, :]).then_inc(s_out, 16)
            sp.wait_ge(s_out, 16 * (len(STORES) - 1))

        @block.gpsimd
        def _(pool):
            pool.memset(wfeat[:, :], 0.0).then_inc(s_zero_node, 1)
            pool.memset(wself_raw, 0.0).then_inc(s_zero_node, 1)
            pool.memset(ident[:, :], 0.0).then_inc(s_ident0, 1)
            pool.wait_ge(s_ident0, 1)
            pool.affine_select(out=ident[:, :], in_=ident[:, :], compare_op=ALU.not_equal, fill=1.0, base=0,
                               pattern=[[-1, 128]], channel_multiplier=1).then_inc(s_ident, 1)
            pool.memset(dst_rows[:, ROWS - 1, :], 0.0).then_inc(s_rows, 1)
            pool.memset(src_rows[:, ROWS - 1, :], 0.0).then_inc(s_rows, 1)
            pool.iota(iota_i[:, :], pattern=[[1, WINDOW]], base=0, channel_multiplier=0).then_inc(s_iota, 1)
            pool.memset(eps_col[:, :], EPS).then_inc(s_iota, 1)
            pool.memset(w1bd[:, :, :], 0.0).then_inc(s_zero, 1)
            pool.memset(w2bd[:, :], 0.0).then_inc(s_zero, 1)
            pool.memset(wpbd[:, :], 0.0).then_inc(s_zero, 1)
            pool.memset(conv_stage[:, :, :], 0.0).then_inc(s_zero, 1)
            pool.wait_ge(s_zero, 4)
            for a in range(8):
                for e in range(2):
                    r = 16 * a + RADIAL * e
                    pool.dma_start(w1bd[r:r + RADIAL, a, HID * e:HID * (e + 1)], W_mlp1).then_inc(s_wts, 16)
            for e in range(2):
                h = slice(HID * e, HID * (e + 1))
                pool.dma_start(w2bd[h, h], W_mlp2).then_inc(s_wts, 16)
                for m in range(4):
                    pool.dma_start(wpbd[h, 128 * e + MUL * m:128 * e + MUL * (m + 1)], Wp[m]).then_inc(s_wts, 16)
            pool.dma_start(conv_stage[0:MUL, 0, 0:MUL], W2_0e[0:MUL, :]).then_inc(s_wts, 16)
            for i in range(3):
                m = slice(MUL * (1 + i), MUL * (2 + i))
                pool.dma_start(conv_stage[m, 0, m], W2_1o[MUL:2 * MUL, :]).then_inc(s_wts, 16)
                pool.dma_start(conv_stage[0:MUL, 1 + i, m], W2_1o[0:MUL, :]).then_inc(s_wts, 16)
                pool.dma_start(conv_stage[m, 1 + i, 0:MUL], W2_0e[MUL:2 * MUL, :]).then_inc(s_wts, 16)

            def gather(s, c):
                for t in range(CT * c, CT * (c + 1)):
                    pool.indirect_dma_start(out=gath[:, s, t, :], out_offset=None, in_=table[:, :],
                                            in_offset=bass.IndirectOffsetOnAxis(ap=idx[:, s, t:t + 1], axis=0))\
                        .then_inc(s_g[s][c], 16)

            def table_stored():
                pool.wait_ge(s_tab[0], 16 * -(-PIECES // 2))
                pool.wait_ge(s_tab[1], 16 * (PIECES // 2))

            table_stored()
            pool.wait_ge(s_flag, 1)
            flag = pool.value_load(flag_i[0:1, 0:1], min_val=0, max_val=NODES)
            with pool.If(flag < WINDOW):
                for b in range(SLOTS):
                    pool.wait_ge(s_idx, b + 1)
                    for c in range(CHUNKS):
                        gather(b, c)
                with pool.Fori(1, QUADS) as n:
                    for s in range(SLOTS):
                        pool.wait_ge(s_idx, n * SLOTS + (s + 1))
                        pool.sem_inc(s_round, 1)
                        for c in range(CHUNKS):
                            gather(s, c)
                for b in (BLOCKS - 2, BLOCKS - 1):
                    pool.wait_ge(s_idx, b + 1)
                    for c in range(CHUNKS):
                        if b < BLOCKS - 1 or c >= CUT // 2:
                            gather(b % SLOTS, c)
            with pool.Else():
                with pool.Fori(0, BLOCKS) as b:
                    pool.wait_ge(s_idx, b + 1)
                    pool.sem_inc(s_round, 1)
                    for c in range(CHUNKS):
                        gather(0, c)

        @block.scalar
        def _(act):
            act.wait_ge(s_zero_node, 2)
            act.dma_start(wfeat[0:MUL, 0:MUL], W1_0e[:, 0:MUL]).then_inc(s_node_w, 16)
            act.dma_start(wself_raw[0:MUL, 0:MUL], W1_0e[:, MUL:2 * MUL]).then_inc(s_node_w, 16)
            for i in range(3):
                cols = slice(MUL * (1 + i), MUL * (2 + i))
                act.dma_start(wfeat[MUL + i:128:3, cols], W1_1o[:, 0:MUL]).then_inc(s_node_w, 16)
                act.dma_start(wself_raw[MUL + i:128:3, cols], W1_1o[:, MUL:2 * MUL]).then_inc(s_node_w, 16)
            for n in range(NODE_BATCHES):
                act.wait_ge(s_xt, n + 1)
                act.copy(acc_v[:, :, BATCH * n:BATCH * (n + 1)].rearrange("q p j -> q j p"),
                         bank[n % 2][:, 0:BATCH * NODE_P].rearrange("q (j p) -> q j p", j=BATCH)).then_inc(s_xts, 1)

            def copy_indices(b, s):
                return act.copy(idx[:, s, :], src_all[:, bass.ds(b * TILES, TILES)])

            def copy_attributes():
                for c in range(ROWS):
                    r = rows_of(c)
                    dest = ea_all[:, 1024 * c:1024 * c + 8 * r].rearrange("q (g e k) -> q e k g", e=2, k=4)
                    for e in range(2):
                        act.wait_ge(s_et, 2 * c + e + 1)
                        act.copy(dest[:, e], bank[6 + e][:, :].rearrange("q (k g) -> q k g", k=4)[:, :, 0:r])\
                            .then_inc(s_ets, 1)

            def gelu1(b, h):
                act.wait_ge(s_h1p[h], b + 1)
                act.activation(h1[:, h, :], hid_ps[h][:, :], ACT.Gelu_apprx_tanh,
                               scale=1.0 / math.sqrt(RADIAL)).then_inc(s_h1[h], 1)

            def gelu2(b, m, h):
                act.wait_ge(s_h2p[h], b + 1)
                act.activation(h2[:, m % 2, :, 4 * h:4 * (h + 1)].rearrange("p e a -> p a e"),
                               hid_ps[h][:, :].rearrange("p (a e) -> p a e", a=4), ACT.Gelu_apprx_tanh,
                               scale=1.0 / math.sqrt(HID)).then_inc(s_h2[h], 1)

            def copy_e8T(b):
                act.wait_ge(s_tr, b + 1)
                act.copy(e8T[:, :], t_ps).then_inc(s_e8T, 1)

            def copy_sums(b):
                act.wait_ge(s_seg[CHUNKS - 1], b + 1)
                act.copy(zsb[:, :], z_ps[:, :]).then_inc(s_zc, 1)

            def step(b, m, first=False, last=False):
                if not last:
                    copy_e8T(b + 1)
                    gelu1(b + 1, 0)
                    gelu1(b + 1, 1)
                if not first:
                    copy_sums(b - 1)
                if not last and not first:
                    copy_indices(b + (SLOTS - 1), (m + SLOTS - 1) % SLOTS).then_inc(s_idx, 1)
                if not last:
                    gelu2(b + 1, m + 1, 0)
                    gelu2(b + 1, m + 1, 1)

            act.wait_ge(s_flag, 1)
            flag = act.value_load(flag_i[0:1, 0:1], min_val=0, max_val=NODES)
            act.wait_ge(s_rts, 2)
            with act.If(flag < WINDOW):
                for b in range(SLOTS):
                    copy_indices(b, b).then_inc(s_idx, 1)
                copy_attributes()
                act.wait_ge(s_rts, 2 * ROWS)
                copy_e8T(0)
                gelu1(0, 0)
                gelu1(0, 1)
                gelu2(0, 0, 0)
                gelu2(0, 0, 1)
                step(0, 0, first=True)
                with act.Fori(0, QUADS) as n:
                    for s in range(1, SLOTS + 1):
                        step(n * SLOTS + s, s)
                step(BLOCKS - 1, BLOCKS - 1, last=True)
                copy_sums(BLOCKS - 1)
            with act.Else():
                copy_attributes()
                act.wait_ge(s_rts, 2 * ROWS)
                with act.Fori(0, BLOCKS) as b:
                    act.wait_ge(s_gblk, b + 0)
                    copy_indices(b, 0).then_inc(s_idx, 1)
                    copy_e8T(b)
                    gelu1(b, 0)
                    gelu1(b, 1)
                    gelu2(b, 0, 0)
                    gelu2(b, 0, 1)
                    for g in range(GROUPS):
                        act.wait_ge(s_gz, b * GROUPS + (g + 1))
                        for e in range(2):
                            last = act.copy(gen_z[:, e], bank[4 + e][:, :].rearrange("p (k n) -> p k n", k=4))
                        last.then_inc(s_gzc, 1)
            for n in range(NORM_BATCHES + 1):
                if n < NORM_BATCHES:
                    act.wait_ge(s_var, n + 1)
                    if n >= 4:
                        act.wait_ge(s_yr, NORM * (n - 3))
                    act.activation(rstd[0:NODE_P, n % 4, 0:norm_tiles(n), 0], moments[0:NODE_P, n % 4, 0:norm_tiles(n), 1],
                                   ACT.Sqrt, bias=eps_col[0:NODE_P, :]).then_inc(s_std, 1)
                if n >= 1:
                    act.wait_ge(s_sc, n)
                    for j in range(norm_tiles(n - 1)):
                        act.activation(x_rows[:, NORM * (n - 1) + j, :], norm_ps(n - 1, j), ACT.Identity,
                                       bias=rstd[0:NODE_P, (n - 1) % 4, j, 1:2],
                                       scale=rstd[0:NODE_P, (n - 1) % 4, j, 0:1]).then_inc(s_yr, 1)

        @block.tensor
        def _(pe):
            pe.wait_ge(s_ident, 1)
            def transpose_x(n):
                pe.wait_ge(s_x[next(i for i in range(len(LOADS)) if LOADS[i + 1] > BATCH * n)], 16)
                if n >= 2:
                    pe.wait_ge(s_xts, n - 1)
                for j in range(BATCH):
                    last = pe.transpose(bank[n % 2][:, NODE_P * j:NODE_P * (j + 1)], x_rows[:, BATCH * n + j, :],
                                        ident[0:NODE_P, 0:NODE_P])
                last.then_inc(s_xt, 1)

            def transpose_indices(c):
                r = rows_of(c)
                pe.wait_ge(s_src_f, c + 1)
                if c >= 2:
                    pe.wait_ge(s_rts, 2 * (c - 1))
                for k, rows in enumerate((src_rows, dst_rows)):
                    for e in range(2):
                        at = 256 * k + 128 * e
                        last = pe.transpose(bank[4 + c % 2][:, at:at + r], rows[0:r, c, e:256:2], ident[0:r, 0:r])
                last.then_inc(s_rt, 1)

            transpose_x(0)
            for n in range(NODE_BATCHES):
                if n + 1 < NODE_BATCHES:
                    transpose_x(n + 1)
                if n == 0:
                    pe.wait_ge(s_wnode, 3)
                pe.wait_ge(s_xts, n + 1)
                if n >= 2:
                    pe.wait_ge(s_feats, n - 1)
                for j in range(BATCH):
                    last = pe.matmul(bank[2 + n % 2][0:NODE_P, 128 * j:128 * (j + 1)], acc_v[:, :, BATCH * n + j],
                                     wfeat[:, :], start=True, stop=True)
                last.then_inc(s_featp, 1)
                if n == OFFSETS_FROM + ROWS:
                    pe.wait_ge(s_base, 1)
                    pe.transpose(bank[7][0:ROWS, 0:128], base_f[:, :], ident[:, :])
                    pe.transpose(bank[7][0:1, 128:256], relmax[:, ROWS:ROWS + 1], ident[:, :]).then_inc(s_small, 1)
                    transpose_indices(0)
            for c in range(1, ROWS):
                transpose_indices(c)
            for n in range(NODE_BATCHES):
                if n >= 2:
                    pe.wait_ge(s_inits, n - 1)
                pe.matmul(bank[2 + n % 2][:, 0:INIT], winit[:, :], acc[:, INIT * n:INIT * (n + 1)],
                          start=True, stop=True).then_inc(s_initp, 1)
                if n % 2 == 0:
                    c = n // 2
                    r = rows_of(c)
                    if c == 0:
                        pe.wait_ge(s_flag, 1)
                        pe.wait_ge(s_base13, 1)
                    pe.wait_ge(s_ea[c % 2], 16 * (c // 2 + 1) if c < WHOLE else 16 * (c // 2 + INDEX_LOADS))
                    for e in range(2):
                        if c >= 1:
                            pe.wait_ge(s_ets, 2 * (c - 1) + e + 1)
                        for k in range(4):
                            last = pe.transpose(bank[6 + e][:, 128 * k:128 * k + r],
                                                ea_rows[0:r, c % 2, 4 * e + k:4 * GROUP:8], ident[0:r, 0:r])
                        last.then_inc(s_et, 1)
            pe.wait_ge(s_inits, NODE_BATCHES)
            pe.wait_ge(s_rts, 2 * ROWS)
            pe.wait_ge(s_ets, 2 * ROWS)
            pe.wait_ge(s_flag, 1)
            pe.wait_ge(s_wts, 16 * LOOP_WEIGHT_LOADS)
            pe.wait_ge(s_conv, 3)

            def transpose_e8(b, s, round_):
                pe.wait_ge(s_e8[s], round_ * 16 + 16)
                pe.wait_ge(s_h2[0], b + 0)
                pe.transpose(t_ps, e8[:, s, :], ident[:, :]).then_inc(s_tr, 1)

            def layer1(b, h, free=None):
                if h == 0:
                    pe.wait_ge(s_e8T, b + 1)
                if free is not None:
                    pe.wait_ge(s_h2[h], free)
                for a in range(4 * h, 4 * h + 4):
                    last = pe.matmul(hid_ps[h][:, 128 * (a % 4):128 * (a % 4 + 1)], w1bd[:, a, :], e8T[:, :],
                                     start=True, stop=True)
                last.then_inc(s_h1p[h], 1)

            def layer2(b, h):
                pe.wait_ge(s_h1[h], b + 1)
                pe.matmul(hid_ps[h][:, :], w2bd[:, :], h1[:, h, :], start=True, stop=True).then_inc(s_h2p[h], 1)

            def radial(b, m, c, first=False):
                if c == 0:
                    pe.wait_ge(s_h2[0], b + 1)
                    pe.wait_ge(s_h2[1], b + 1)
                if not first:
                    pe.wait_ge(s_prod[c], b)
                for r in range(2):
                    g = 2 * c + r
                    last = pe.matmul(wgt_ps[c][:, 256 * r:256 * (r + 1)],
                                     h2[:, m % 2, 16 * g:16 * (g + 1), :].rearrange("p e a -> p (e a)"), wpbd[:, :],
                                     start=True, stop=True)
                last.then_inc(s_w[c], 1)

            def segment_sum(b, m, c, first=False):
                if c == 0:
                    pe.wait_ge(s_sel, b + 1)
                    if not first:
                        pe.wait_ge(s_zc, b + 0)
                pe.wait_ge(s_prod[c], b + 1)
                for r in range(2):
                    g = 2 * c + r
                    for half, at, n in ((0, 0, 1), (1, WINDOW, 3)):
                        o = 4 * WINDOW * g + at
                        for e in range(2):
                            last = pe.matmul(z_ps[:, o:o + n * WINDOW],
                                             prod[:, c, 2 * r + e, 128 * half:128 * (half + 1)],
                                             sel[:, m % 2, 2 * g + e, half:half + n, :], start=(e == 0), stop=(e == 1))
                last.then_inc(s_seg[c], 1)

            def convolve(b):
                pe.wait_ge(s_zc, b + 1)
                pe.wait_ge(s_add[GROUPS - 1], b + 0)
                for k in range(4):
                    last = pe.matmul(y_ps, conv[:, k, :],
                                     zsb[:, :].rearrange("p (g k w) -> p g k w", g=GROUPS, k=4)[:, :, k, :],
                                     start=(k == 0), stop=(k == 3))
                last.then_inc(s_y, 1)

            def step(b, m, round_, first=False, last=False):
                for c in range(CHUNKS):
                    if c == 0 and not last:
                        transpose_e8(b + 1, (m + 1) % SLOTS, round_)
                    radial(b, m, c, first)
                    if not last:
                        if c < 2:
                            layer1(b + 1, c, b + 1)
                        else:
                            layer2(b + 1, c - 2)
                    if c >= 2:
                        segment_sum(b, m, c - 2, first)
                    elif not first:
                        segment_sum(b - 1, m - 1, c + 2)
                    if c == 2 and not first:
                        convolve(b - 1)

            flag = pe.value_load(flag_i[0:1, 0:1], min_val=0, max_val=NODES)
            with pe.If(flag < WINDOW):
                transpose_e8(0, 0, 0)
                layer1(0, 0)
                layer1(0, 1)
                layer2(0, 0)
                layer2(0, 1)
                step(0, 0, 0, first=True)
                with pe.Fori(0, QUADS) as n:
                    for s in range(1, SLOTS + 1):
                        step(n * SLOTS + s, s, n + (s + 1) // SLOTS)
                step(BLOCKS - 1, BLOCKS - 1, 0, last=True)
                segment_sum(BLOCKS - 1, BLOCKS - 1, 2)
                segment_sum(BLOCKS - 1, BLOCKS - 1, 3)
                convolve(BLOCKS - 1)
                pe.wait_ge(s_add[GROUPS - 1], BLOCKS)
            with pe.Else():
                with pe.Fori(0, BLOCKS) as b:
                    transpose_e8(b, 0, b)
                    layer1(b, 0)
                    layer1(b, 1)
                    layer2(b, 0)
                    layer2(b, 1)
                    pe.wait_ge(s_h2[0], b + 1)
                    pe.wait_ge(s_h2[1], b + 1)
                    for g in range(GROUPS):
                        pe.wait_ge(s_gprod, b * GROUPS + g)
                        pe.matmul(wgt_ps[0][:, 0:256], h2[:, 0, 16 * g:16 * (g + 1), :].rearrange("p e a -> p (e a)"),
                                  wpbd[:, :], start=True, stop=True).then_inc(s_gw, 1)
                        pe.wait_ge(s_gdiag, b * GROUPS + (g + 1))
                        pe.wait_ge(s_gprod, b * GROUPS + (g + 1))
                        for e in range(2):
                            for half, n in ((0, 1), (1, 3)):
                                last = pe.matmul(bank[4 + e][:, 128 * half:128 * (half + n)],
                                                 prod[:, 0, e, 128 * half:128 * (half + 1)],
                                                 diag[:, e, half:half + n, :], start=True, stop=True)
                        last.then_inc(s_gz, 1)
                        pe.wait_ge(s_gzc, b * GROUPS + (g + 1))
                        for k in range(4):
                            last = pe.matmul(z_ps[:, 0:256], conv[:, k, :], gen_z[:, :, k, :],
                                             start=(k == 0), stop=(k == 3))
                        last.then_inc(s_gy, 1)
                    pe.wait_ge(s_gblk, b + 1)
            for n in range(NORM_BATCHES):
                if n >= 4:
                    pe.wait_ge(s_yr, NORM * (n - 3))
                for j in range(norm_tiles(n)):
                    last = pe.transpose(norm_ps(n, j), acc_v[:, :, NORM * n + j], ident[:, :])
                last.then_inc(s_ft, 1)

        @block.vector
        def _(dve):
            links = [0]

            def link(instruction):
                links[0] += 1
                instruction.then_inc(s_prep, 1)
                dve.wait_ge(s_prep, links[0])

            dve.wait_ge(s_node_w, 16 * NODE_WEIGHT_LOADS)
            dve.wait_ge(s_ident, 1)
            dve.tensor_scalar(wfeat[:, :], wfeat[:, :], FEAT_SCALE, None, ALU.mult).then_inc(s_wnode, 1)
            dve.scalar_tensor_tensor(winit[:, 0:MUL], wself_raw[:, 0:MUL], SELF_SCALE, ident[:, 0:MUL],
                                     ALU.mult, ALU.add).then_inc(s_wnode, 1)
            by_unit = lambda ap: ap.rearrange("p (w i) -> p i w", i=3)
            dve.scalar_tensor_tensor(by_unit(winit[:, MUL:128]), wself_raw[:, MUL:128].rearrange("p (i w) -> p i w", i=3),
                                     SELF_SCALE, by_unit(ident[:, MUL:128]), ALU.mult, ALU.add).then_inc(s_wnode, 1)
            dve.wait_ge(s_iota, 2)
            dve.tensor_copy(iota_w[:, :], iota_i[:, :]).then_inc(s_wnode, 1)
            dve.memset(src_all[:, ALL_GROUPS * 2:], 0).then_inc(s_wnode, 1)
            dve.memset(acc[:, NODES:], 0.0).then_inc(s_wnode, 1)

            dst_i, src_i = dst_rows.bitcast(INT32), src_rows.bitcast(INT32)

            def offsets(c):
                link(dve.tensor_reduce(base_f[:, c:c + 1], dst_i[:, c, :], AXIS_X, ALU.min))
                link(dve.tensor_scalar(dst_rows[:, c, :], dst_i[:, c, :], base_f[:, c:c + 1], None, ALU.subtract))
                link(dve.tensor_reduce(relmax[:, c:c + 1], dst_rows[:, c, :], AXIS_X, ALU.max))

            def copy_indices_back(c):
                r = rows_of(c)
                dve.wait_ge(s_rt, c + 1)
                ps = bank[4 + c % 2][:, :].rearrange("q (k e g) -> q k e g", k=2, e=2)
                for k, every in enumerate((src_all, rel_all)):
                    dve.tensor_copy(every[:, 256 * c:256 * c + 2 * r].rearrange("q (g e) -> q e g", e=2),
                                    ps[:, k, :, 0:r]).then_inc(s_rts, 1)

            per_piece = PIECE // BATCH
            for n in range(NODE_BATCHES):
                piece = n // per_piece
                dve.wait_ge(s_featp, n + 1)
                if n % per_piece == 0 and piece >= 2:
                    dve.wait_ge(s_tab[piece % 2], 16 * (piece // 2))
                j = BATCH * (n % per_piece)
                dve.tensor_copy(feat_rows[:, piece % 2, j:j + BATCH, :],
                                bank[2 + n % 2][0:NODE_P, :].rearrange("p (j f) -> p j f", j=BATCH)).then_inc(s_feats, 1)
                if OFFSETS_FROM <= n < OFFSETS_FROM + ROWS:
                    if n == OFFSETS_FROM:
                        dve.wait_ge(s_dst, 16 * INDEX_LOADS)
                    offsets(n - OFFSETS_FROM)
                if n == OFFSETS_FROM + ROWS - 1:
                    dve.tensor_reduce(relmax[:, ROWS:ROWS + 1], relmax[:, 0:ROWS], AXIS_X, ALU.max).then_inc(s_base, 1)
                    dve.wait_ge(s_src, 16 * INDEX_LOADS)
                    dve.tensor_copy(src_rows[:, 0, :], src_i[:, 0, :]).then_inc(s_src_f, 1)
                if n == OFFSETS_FROM + ROWS + 2:
                    dve.wait_ge(s_small, 1)
                    dve.tensor_reduce(flag_i[0:1, 0:1], bank[7][0:1, 128:256], AXIS_X, ALU.max).then_inc(s_flag, 1)
                    dve.tensor_copy(base13[:, :], bank[7][0:ROWS, 0:128]).then_inc(s_base13, 1)
                    copy_indices_back(0)
            for c in range(1, ROWS):
                dve.tensor_copy(src_rows[:, c, :], src_i[:, c, :]).then_inc(s_src_f, 1)
            for c in range(1, ROWS):
                copy_indices_back(c)
            for n in range(NODE_BATCHES):
                dve.wait_ge(s_initp, n + 1)
                dve.tensor_copy(acc[:, INIT * n:INIT * (n + 1)], bank[2 + n % 2][:, 0:INIT]).then_inc(s_inits, 1)
                if n == NODE_BATCHES - 3:
                    dve.wait_ge(s_et, 2 * (ROWS - 2))
                    dve.memset(ea_rows[:, (ROWS - 1) % 2, :], 0.0).then_inc(s_eaz, 1)
            dve.wait_ge(s_wts, 16 * LOOP_WEIGHT_LOADS)
            dve.tensor_scalar(conv[:, :, MUL:128].rearrange("p k (w i) -> p k i w", i=3),
                              conv_stage[:, :, MUL:128].rearrange("p k (i w) -> p k i w", i=3),
                              CONV_SCALE, None, ALU.mult).then_inc(s_conv, 1)
            dve.tensor_scalar(conv[:, 0, 0:MUL], conv_stage[:, 0, 0:MUL], CONV_SCALE, None, ALU.mult).then_inc(s_conv, 1)
            dve.tensor_scalar(conv[:, 1:4, 0:MUL], conv_stage[:, 1:4, 0:MUL], CONV_SCALE * INV_SQRT3, None,
                              ALU.mult).then_inc(s_conv, 1)
            dve.wait_ge(s_ets, 2 * ROWS)
            dve.wait_ge(s_inits, NODE_BATCHES)

            def select(b, m, free=None):
                ts_ = bass.ds(b * TILES, TILES)
                if free is not None:
                    dve.wait_ge(s_seg[CHUNKS - 1], free)
                dve.wait_ge(s_sel, b + 0)
                dve.tensor_tensor(sel01[:, :, :], rel_all[:, ts_].unsqueeze(2).to_broadcast([128, TILES, WINDOW]),
                                  iota_w[:, :].unsqueeze(1).to_broadcast([128, TILES, WINDOW]),
                                  ALU.is_equal).then_inc(s_sel0, 1)
                dve.wait_ge(s_sel0, b + 1)
                attr = ea_all[:, bass.ds(b * (TILES * 4), TILES * 4)].rearrange("q (t k) -> q t k", k=4)
                dve.tensor_tensor(sel[:, m % 2], sel01[:, :, :].unsqueeze(2).to_broadcast([128, TILES, 4, WINDOW]),
                                  attr.unsqueeze(3).to_broadcast([128, TILES, 4, WINDOW]), ALU.mult).then_inc(s_sel, 1)

            def multiply(weights, rows, to, n):
                w = weights.rearrange("q (t h a u) -> q t h a u", t=n, h=2, a=2)
                f = rows.rearrange("q t (s u) -> q t s u", s=4)
                o = to.rearrange("q t (h s u) -> q t h s u", h=2, s=4)
                dve.tensor_tensor(o[:, :, :, 0, :], w[:, :, :, 0, :],
                                  f[:, :, 0, :].unsqueeze(2).to_broadcast([128, n, 2, MUL]), ALU.mult)
                for h in range(2):
                    last = dve.tensor_tensor(o[:, :, h, 1:4, :],
                                             w[:, :, h, 1, :].unsqueeze(2).to_broadcast([128, n, 3, MUL]),
                                             f[:, :, 1:4, :], ALU.mult)
                return last

            def products(b, m, c, round_, first=False):
                dve.wait_ge(s_w[c], b + 1)
                dve.wait_ge(s_g[m % SLOTS][c], round_ * (16 * CT) + 16 * CT)
                if not first:
                    dve.wait_ge(s_seg[c], b)
                multiply(wgt_ps[c][:, :], gath[:, m % SLOTS, CT * c:CT * (c + 1), :], prod[:, c], CT).then_inc(s_prod[c], 1)

            def add_windows(b):
                _, base = nc.values_load_multi_w_load_instructions(
                    base_row[0:1, bass.ds(b * GROUPS, GROUPS)], engines=(mybir.EngineType.DVE,),
                    min_val=0, max_val=NODES - 1,
                    skip_runtime_bounds_check_because="a destination is a node's number by the kernel's contract")
                dve.wait_ge(s_y, b + 1)
                for g in range(GROUPS):
                    if g:
                        dve.wait_ge(s_add[g - 1], b + 1)
                    else:
                        dve.wait_ge(s_add[GROUPS - 1], b + 0)
                    at = bass.ds(base[g], WINDOW)
                    dve.tensor_tensor(acc[:, at], acc[:, at], y_ps[:, WINDOW * g:WINDOW * (g + 1)], ALU.add)\
                        .then_inc(s_add[g], 1)

            def step(b, m, round_, first=False, last=False):
                for c in range(CHUNKS):
                    if c == 2 and not last:
                        select(b + 1, m + 1, None if first else b)
                    products(b, m, c, round_ - (last and c < CUT // 2), first)
                if not first:
                    add_windows(b - 1)

            flag = dve.value_load(flag_i[0:1, 0:1], min_val=0, max_val=NODES)
            dve.wait_ge(s_br, 16)
            with dve.If(flag < WINDOW):
                select(0, 0)
                step(0, 0, 0, first=True)
                with dve.Fori(0, QUADS) as n:
                    for s in range(1, SLOTS + 1):
                        step(n * SLOTS + s, s, n + s // SLOTS)
                step(BLOCKS - 1, BLOCKS - 1, (BLOCKS - 1) // SLOTS, last=True)
                add_windows(BLOCKS - 1)
            with dve.Else():
                def general_block(b, start):
                    for c in range(CHUNKS):
                        dve.wait_ge(s_g[0][c], b * (16 * CT) + 16 * CT)
                    for g in range(GROUPS):
                        for e in range(2):
                            attr = ea_all[:, bass.ds(b * (TILES * 4) + 4 * (2 * g + e), 4)]
                            last = dve.tensor_tensor(diag[:, e], ident[:, :].unsqueeze(1).to_broadcast([128, 4, 128]),
                                                     attr.unsqueeze(2).to_broadcast([128, 4, 128]), ALU.mult)
                        last.then_inc(s_gdiag, 1)
                        dve.wait_ge(s_gw, b * GROUPS + (g + 1))
                        multiply(wgt_ps[0][:, 0:256], gath[:, 0, 2 * g:2 * g + 2, :], prod[:, 0, 0:2], 2)\
                            .then_inc(s_gprod, 1)
                        columns = z_ps[:, 0:256].rearrange("f (e n) -> f n e", e=2)
                        dve.sem_clear(s_gadd)
                        with dve.Fori(0, GROUP // 4) as n:
                            _, node = nc.values_load_multi_w_load_instructions(
                                dst[bass.ds(start + GROUP * g + n * 4, 4)].rearrange("(a n) -> a n", a=1),
                                engines=(mybir.EngineType.DVE,), min_val=0, max_val=NODES - 1)
                            dve.wait_ge(s_gy, b * GROUPS + (g + 1))
                            for k in range(4):
                                dve.wait_ge(s_gadd, n * 4 + k)
                                at = bass.ds(node[k], 1)
                                dve.tensor_tensor(acc[:, at], acc[:, at], columns[:, bass.ds(n * 2 + k // 2, 1), k % 2],
                                                  ALU.add).then_inc(s_gadd, 1)
                        dve.wait_ge(s_gadd, GROUP)
                    dve.memset(flag_i[0:1, 1:2], 0).then_inc(s_gblk, 1)

                with dve.Fori(0, BLOCKS - 1) as b:
                    general_block(b, b * BLOCK)
                general_block(BLOCKS - 1, LAST_START)

            def moments_of(n):
                dve.wait_ge(s_ft, n + 1)
                for j in range(norm_tiles(n)):
                    last = dve.bn_stats(stats[0:NODE_P, n % 4, j, :], norm_ps(n, j))
                link(last)
                for j in range(norm_tiles(n)):
                    last = dve.bn_aggr(moments[0:NODE_P, n % 4, j, :], stats[0:NODE_P, n % 4, j, :])
                last.then_inc(s_var, 1)

            def scales_of(n):
                dve.wait_ge(s_std, n + 1)
                r = rstd[0:NODE_P, n % 4, 0:norm_tiles(n), :]
                link(dve.reciprocal(r[:, :, 0], r[:, :, 0]))
                dve.scalar_tensor_tensor(r[:, :, 1], moments[0:NODE_P, n % 4, 0:norm_tiles(n), 0], -1.0, r[:, :, 0],
                                         ALU.mult, ALU.mult).then_inc(s_sc, 1)

            for n in range(NORM_BATCHES + 1):
                if n < NORM_BATCHES:
                    moments_of(n)
                if n >= 1:
                    scales_of(n - 1)
    return nc


_INS = ['x', 'src', 'dst', 'edge_attr_4', 'edge_attr_8', 'L0_gnn_W1_0e', 'L0_gnn_W1_1o', 'L0_gnn_W_mlp1',
        'L0_gnn_W_mlp2', 'L0_gnn_Wp_00', 'L0_gnn_Wp_01', 'L0_gnn_Wp_10', 'L0_gnn_Wp_11', 'L0_gnn_W2_0e', 'L0_gnn_W2_1o']


def kernel(**inputs):
    import numpy as np
    import concourse.bacc as bacc
    from concourse.bass_utils import run_bass_kernel_spmd

    nc = bacc.Bacc("TRN2", target_bir_lowering=False, num_devices=1)
    arrays, aps = {}, {}
    for name in _INS:
        a = np.ascontiguousarray(inputs[name])
        arrays[f"in_{name}"] = a
        aps[name] = nc.dram_tensor(f"in_{name}", a.shape, mybir.dt.from_np(a.dtype), kind="ExternalInput").ap()
    out = nc.dram_tensor("out_0", (NODES, FEAT), FP32, kind="ExternalOutput").ap()
    w = {name.removeprefix("L0_gnn_"): aps[name] for name in _INS[5:]}
    build_program(nc, aps['x'], aps['src'], aps['dst'], aps['edge_attr_4'], aps['edge_attr_8'], w['W1_0e'], w['W1_1o'],
                  w['W_mlp1'], w['W_mlp2'], [w['Wp_00'], w['Wp_10'], w['Wp_01'], w['Wp_11']], w['W2_0e'], w['W2_1o'], out)
    r = run_bass_kernel_spmd(nc, [arrays], core_ids=[0])
    return r.results[0]["out_0"]
```

```python
import math

import concourse.bass as bass
from concourse import mybir
from contextlib import ExitStack

FP32 = mybir.dt.float32
INT32 = mybir.dt.int32
INT16 = mybir.dt.int16
BF16 = mybir.dt.bfloat16
ALU = mybir.AluOpType
ACT = mybir.ActivationFunctionType
AXIS_X = mybir.AxisListType.X

NODES, FEAT, EDGES = 12500, 128, 412500
MUL, RADIAL, HID = 32, 8, 64
NODE_P = 125
NODE_J = NODES // NODE_P
BATCH = 4
NODE_BATCHES = NODE_J // BATCH
LOADS = (0, 4, 12, 20, 40, 60, 80, 100)
TABLE_CUTS = (0, 20, 40, 60, 80, 92, 100)
PIECE = max(b - a for a, b in zip(TABLE_CUTS, TABLE_CUTS[1:]))
PIECES = len(TABLE_CUTS) - 1
PIECE_SLOTS = 3
STORES = (0, 20, 40, 60, 80, 92, 100)
NORM = 8
NORM_BATCHES = -(-NODE_J // NORM)
GROUP = 256
BLOCK = 2048
GROUPS = BLOCK // GROUP
TILES = BLOCK // 128
CHUNKS = 4
CT = TILES // CHUNKS
BLOCKS = -(-EDGES // BLOCK)
LAST_START = EDGES - BLOCK
OVERLAP = BLOCKS * BLOCK - EDGES
ALL_GROUPS = BLOCKS * GROUPS
ROWS = -(-ALL_GROUPS // 128)
WINDOW = 16
EA_SLOTS = 8
SLOTS = 4
QUADS = (BLOCKS - 2) // SLOTS
assert BLOCKS == 2 + SLOTS * QUADS

MIX = math.pi / 8.0
SELF_SCALE = math.cos(MIX) / math.sqrt(MUL)
FEAT_SCALE = 1.0 / math.sqrt(MUL)
CONV_SCALE = math.sin(MIX) / math.sqrt(2.0) / math.sqrt(32.0) / math.sqrt(2.0 * MUL)
INV_SQRT3 = 1.0 / math.sqrt(3.0)
EPS = 1e-05


def rows_of(c):
    return min(128, ALL_GROUPS - 128 * c)


def build_program(nc, x, src, dst, ea4, ea8, W1_0e, W1_1o, W_mlp1, W_mlp2, Wp, W2_0e, W2_1o, out):
    ctx = ExitStack()
    with ctx:
        def sb(name, shape, dt=FP32):
            return ctx.enter_context(nc.sbuf_tensor(name, shape, dt))

        def sem(name):
            return ctx.enter_context(nc.semaphore(name))

        table = nc.dram_tensor("feature_table", [NODES, FEAT], FP32, kind="Internal").ap()
        base_dram = nc.dram_tensor("group_bases", [ROWS, 128], INT32, kind="Internal").ap()

        acc = sb("acc", [128, NODES + WINDOW])
        ea_all = sb("ea_all", [128, ALL_GROUPS * 2 * 4])
        rel_all = sb("rel_all", [128, ALL_GROUPS * 2], BF16)
        src_all = sb("src_all", [128, (BLOCKS + 2) * TILES], INT16)
        gath = sb("gath", [128, SLOTS, TILES, FEAT])
        idx = sb("idx", [128, SLOTS, TILES], INT32)
        e8 = sb("e8", [128, SLOTS, 128])
        e8T = sb("e8T", [128, 128])
        zsb = sb("zsb", [128, GROUPS * 4 * WINDOW])
        ident = sb("ident", [128, 128])
        iota_i = sb("iota_i", [128, WINDOW], INT32)
        iota_w = sb("iota_w", [128, WINDOW], BF16)
        w1bd = sb("w1bd", [128, 8, 128])
        w2bd = sb("w2bd", [128, 128])
        wpbd = sb("wpbd", [128, 2 * 128])
        wfeat = sb("wfeat", [128, 128])
        winit = sb("winit", [128, 128])
        conv = sb("conv", [128, 4, 128])
        base_f = sb("base_f", [128, ROWS])
        relmax = sb("relmax", [128, ROWS + 1])
        base13 = sb("base13", [ROWS, 128], INT32)
        base_row = sb("base_row", [1, ROWS * 128], INT32)
        flag_i = sb("flag_i", [1, 8], INT32)
        stats = sb("stats", [128, 4, NORM, 6])
        moments = sb("moments", [128, 4, NORM, 2])
        rstd = sb("rstd", [128, 4, NORM, 2])
        eps_col = sb("eps_col", [128, 1])

        work = sb("work", [128, 9216])
        prod = work[:, 0:4096].rearrange("p (c t f) -> p c t f", c=CHUNKS, t=CT)
        sel = work[:, 4096:6144].rearrange("p (b t k w) -> p b t k w", b=2, t=TILES, k=4)
        h1 = work[:, 6144:7168].rearrange("p (h n) -> p h n", h=2)
        h2 = work[:, 7168:9216].rearrange("p (b e a) -> p b e a", b=2, a=8)
        ea_rows = work[:, 0:EA_SLOTS * 1024].rearrange("p (b e) -> p b e", b=EA_SLOTS)
        dst_rows = work[:, 2048:2048 + ROWS * 256].rearrange("p (c e) -> p c e", c=ROWS)
        src_rows = work[:, 2048 + ROWS * 256:2048 + 2 * ROWS * 256].rearrange("p (c e) -> p c e", c=ROWS)
        assert 2 * ROWS * 256 + 2048 <= 9216
        wself_raw = zsb[:, 0:128]
        x_rows = ea_all[0:NODE_P, 0:NODE_J * FEAT].rearrange("p (j d) -> p j d", d=FEAT)
        feat_rows = gath[0:NODE_P, :, :, :].rearrange("p s t f -> p (s t) f")[:, 0:PIECE_SLOTS * PIECE, :]\
            .rearrange("p (b j) f -> p b j f", b=PIECE_SLOTS)
        sel01 = sb("sel01", [128, TILES, WINDOW])
        conv_stage = sb("conv_stage", [128, 4, 128])
        diag = work[:, 4096:5120].rearrange("p (t k n) -> p t k n", t=2, k=4)
        gen_z = work[:, 3072:4096].rearrange("p (t k n) -> p t k n", t=2, k=4)

        bank = [ctx.enter_context(nc.psum_tensor(f"bank{i}", [128, 512], FP32)) for i in range(8)]
        hid_ps = [bank[0], bank[1]]
        wgt_ps = [bank[2], bank[3], bank[4], bank[5]]
        z_ps = bank[6]
        t_ps = bank[0][:, 0:128]
        y_ps = bank[7][:, 0:128]

        s_node_w = sem("node_weights_in")
        s_x = [sem(f"x_in{i}") for i in range(len(LOADS) - 1)]
        s_rows = sem("index_rows_zeroed")
        s_dst = sem("dst_in")
        s_src0 = sem("first_src_in")
        s_src = sem("src_in")
        s_ea = [sem(f"ea_in{i}") for i in range(EA_SLOTS)]
        s_eaz = sem("ea_tail_zeroed")
        s_zero = sem("weights_zeroed")
        s_zero_node = sem("node_weights_zeroed")
        s_wts_pool = sem("loop_weights_in_pool")
        s_wts_act = sem("loop_weights_in_scalar")
        s_ident0 = sem("ident_zeroed")
        s_ident = sem("ident_ready")
        s_iota = sem("iota_ready")
        s_prep = sem("vector_chain")
        s_wnode = sem("node_weights_ready")
        s_xt = sem("x_transposed")
        s_xts = sem("x_transposed_copied")
        s_featp = sem("features_done")
        s_feats = sem("features_copied")
        s_initp = sem("init_done")
        s_inits = sem("init_copied")
        s_tab = [sem(f"table_stored{i}") for i in range(PIECE_SLOTS)]
        s_src_f = sem("src_as_float")
        s_min = sem("group_minimum_ready")
        s_rel = sem("offsets_ready")
        s_base = sem("bases_ready")
        s_small = sem("small_transposes_done")
        s_base13 = sem("bases_transposed")
        s_bd = sem("bases_in_dram")
        s_br = sem("bases_in_row")
        s_flag = sem("flag_ready")
        s_rt = sem("index_transposes_done")
        s_rts = [sem(f"index_transposes_copied{i}") for i in range(2)]
        s_et = sem("ea_transposes_done")
        s_ets = sem("ea_transposes_copied")
        s_conv = sem("conv_weights_ready")
        s_e8 = [sem(f"e8_in{i}") for i in range(SLOTS)]
        s_tr = sem("e8_transposed")
        s_e8T = sem("e8_transposed_copied")
        s_h1p = [sem(f"layer1_done{h}") for h in range(2)]
        s_h1 = [sem(f"gelu1_done{h}") for h in range(2)]
        s_h2p = [sem(f"layer2_done{h}") for h in range(2)]
        s_h2 = [sem(f"gelu2_done{h}") for h in range(2)]
        s_w = [sem(f"radial_weights_done{c}") for c in range(CHUNKS)]
        s_idx = sem("indices_ready")
        s_g = [[sem(f"gathered{s}_{c}") for c in range(CHUNKS)] for s in range(SLOTS)]
        s_round = sem("gather_slot_seen_free")
        s_sel0 = sem("onehot_ready")
        s_sel = sem("selection_ready")
        s_prod = [sem(f"products_ready{c}") for c in range(CHUNKS)]
        s_seg = [sem(f"segments_summed{c}") for c in range(CHUNKS)]
        s_zc = sem("sums_copied")
        s_y = sem("conv_done")
        s_add = [sem(f"window_added{g}") for g in range(GROUPS)]
        s_gadd = sem("general_edge_added")
        s_gz = sem("general_sums_done")
        s_gzc = sem("general_sums_copied")
        s_gprod = sem("general_products_ready")
        s_gdiag = sem("general_diagonals_ready")
        s_gw = sem("general_weights_done")
        s_gy = sem("general_conv_done")
        s_gblk = sem("general_block_added")
        s_ft = sem("rows_transposed")
        s_var = sem("variance_ready")
        s_std = sem("std_ready")
        s_sc = sem("scale_ready")
        s_yr = sem("rows_normalised")
        s_out = sem("out_stored")

        x_v = x.rearrange("(p j) d -> p j d", j=NODE_J)
        out_v = out.rearrange("(p j) d -> p j d", j=NODE_J)
        table_v = table.rearrange("(p j) d -> p j d", j=NODE_J)
        FULL = (ALL_GROUPS - GROUPS)
        dst_v = dst[0:FULL * GROUP].rearrange("(r e) -> r e", e=GROUP)
        src_v = src[0:FULL * GROUP].rearrange("(r e) -> r e", e=GROUP)
        ea_v = ea4[0:FULL * GROUP, :].rearrange("(r e) c -> r (e c)", e=GROUP)
        dst_t = dst[LAST_START:EDGES].rearrange("(r e) -> r e", e=GROUP)
        src_t = src[LAST_START:EDGES].rearrange("(r e) -> r e", e=GROUP)
        ea_t = ea4[LAST_START:EDGES, :].rearrange("(r e) c -> r (e c)", e=GROUP)
        WHOLE = FULL // 128
        LEFT = FULL - 128 * WHOLE
        CUT, CUT_E = OVERLAP // GROUP, OVERLAP % GROUP
        acc_v = acc[:, 0:NODES].rearrange("q (p j) -> q p j", j=NODE_J)
        INDEX_LOADS = 3
        NODE_WEIGHT_LOADS = 8
        POOL_WEIGHT_LOADS = 14
        WEIGHTS_FROM = 3
        OFFSETS_FROM = 6
        INIT = NODES // NODE_BATCHES
        EARLY_INITS = 6

        def attributes_behind(c):
            return EARLY_INITS + c * 3 // 2

        assert attributes_behind(ROWS - 1) < NODE_BATCHES

        def norm_tiles(n):
            return min(NORM, NODE_J - NORM * n)

        def norm_ps(n, j):
            return bank[2 * (n % 4) + j // 4][0:NODE_P, 128 * (j % 4):128 * (j % 4 + 1)]

        block = ctx.enter_context(nc.Block())

        def index_chunk(c):
            r = rows_of(c)
            ps = bank[4 + c % 2][:, :].rearrange("q (k e g) -> q k e g", k=2, e=2)
            for k, every in enumerate((src_all, rel_all)):
                yield every[:, 256 * c:256 * c + 2 * r].rearrange("q (g e) -> q e g", e=2), ps[:, k, :, 0:r]

        loop_weights = []
        for a in range(8):
            for e in range(2):
                r = 16 * a + RADIAL * e
                loop_weights.append((w1bd[r:r + RADIAL, a, HID * e:HID * (e + 1)], W_mlp1))
        for e in range(2):
            h = slice(HID * e, HID * (e + 1))
            loop_weights.append((w2bd[h, h], W_mlp2))
            for m in range(4):
                loop_weights.append((wpbd[h, 128 * e + MUL * m:128 * e + MUL * (m + 1)], Wp[m]))
        loop_weights.append((conv_stage[0:MUL, 0, 0:MUL], W2_0e[0:MUL, :]))
        for i in range(3):
            m = slice(MUL * (1 + i), MUL * (2 + i))
            loop_weights.append((conv_stage[m, 0, m], W2_1o[MUL:2 * MUL, :]))
            loop_weights.append((conv_stage[0:MUL, 1 + i, m], W2_1o[0:MUL, :]))
            loop_weights.append((conv_stage[m, 1 + i, 0:MUL], W2_0e[MUL:2 * MUL, :]))
        LOOP_WEIGHT_LOADS = len(loop_weights)

        @block.sync
        def _(sp):
            def load_x(n):
                j = slice(LOADS[n], LOADS[n + 1])
                sp.dma_start(x_rows[:, j, :], x_v[:, j, :]).then_inc(s_x[n], 16)

            def load_indices(rows, whole, tail, arrived, c=0):
                r = rows.bitcast(INT32)
                sp.dma_start(r[:, c:WHOLE, :], whole[128 * c:128 * WHOLE, :].rearrange("(c p) e -> p c e", p=128))\
                    .then_inc(arrived, 16)
                sp.dma_start(r[0:LEFT, WHOLE, :], whole[128 * WHOLE:, :]).then_inc(arrived, 16)
                sp.dma_start(r[LEFT:LEFT + GROUPS, WHOLE, :], tail).then_inc(arrived, 16)

            def store_table(n):
                lo, hi = TABLE_CUTS[n], TABLE_CUTS[n + 1]
                sp.wait_ge(s_feats, hi // BATCH)
                sp.dma_start(table_v[:, lo:hi, :], feat_rows[:, n % PIECE_SLOTS, 0:hi - lo, :])\
                    .then_inc(s_tab[n % PIECE_SLOTS], 16)

            load_x(0)
            load_x(1)
            load_x(2)
            sp.wait_ge(s_node_w, 16 * NODE_WEIGHT_LOADS)
            load_x(3)
            sp.wait_ge(s_rows, 2)
            load_indices(dst_rows, dst_v, dst_t, s_dst)
            load_x(4)
            store_table(0)
            load_x(5)
            store_table(1)
            load_x(6)
            store_table(2)
            store_table(3)
            sp.dma_start(src_rows.bitcast(INT32)[:, 0, :], src_v[0:128, :]).then_inc(s_src0, 16)
            for n in range(4, PIECES):
                store_table(n)
            load_indices(src_rows, src_v, src_t, s_src, 1)
            for c in range(ROWS):
                if c == 2:
                    sp.wait_ge(s_rt, ROWS)
                if c >= EA_SLOTS:
                    sp.wait_ge(s_et, 2 * (c - EA_SLOTS + 1))
                if c < WHOLE:
                    sp.dma_start(ea_rows[:, c % EA_SLOTS, :], ea_v[128 * c:128 * (c + 1), :]).then_inc(s_ea[c % EA_SLOTS], 16)
                else:
                    sp.wait_ge(s_eaz, 1)
                    sp.dma_start(ea_rows[0:LEFT, c % EA_SLOTS, :], ea_v[128 * c:, :]).then_inc(s_ea[c % EA_SLOTS], 16)
                    sp.dma_start(ea_rows[LEFT + CUT:LEFT + CUT + 1, c % EA_SLOTS, 4 * CUT_E:], ea_t[CUT:CUT + 1, 4 * CUT_E:])\
                        .then_inc(s_ea[c % EA_SLOTS], 16)
                    sp.dma_start(ea_rows[LEFT + CUT + 1:LEFT + GROUPS, c % EA_SLOTS, :], ea_t[CUT + 1:, :])\
                        .then_inc(s_ea[c % EA_SLOTS], 16)
                if c == 2:
                    sp.wait_ge(s_base13, 1)
                    sp.dma_start(base_dram, base13[:, :]).then_inc(s_bd, 16)
                if c == 4:
                    sp.wait_ge(s_bd, 16)
                    sp.dma_start(base_row[0:1, :], base_dram.rearrange("(a c) p -> a (c p)", a=1)).then_inc(s_br, 16)

            def e8_block(start):
                return ea8[bass.ds(start, BLOCK), :].rearrange("(p j) f -> p (j f)", p=128)

            sp.wait_ge(s_flag, 1)
            flag = sp.value_load(flag_i[0:1, 0:1], min_val=0, max_val=NODES)
            with sp.If(flag < WINDOW):
                for b in range(SLOTS):
                    sp.dma_start(e8[:, b, :], e8_block(b * BLOCK)).then_inc(s_e8[b], 16)
                with sp.Fori(1, QUADS) as n:
                    for s in range(SLOTS):
                        sp.wait_ge(s_tr, n * SLOTS + (s - SLOTS + 1))
                        sp.dma_start(e8[:, s, :], e8_block((n * SLOTS + s) * BLOCK)).then_inc(s_e8[s], 16)
                for b in (BLOCKS - 2, BLOCKS - 1):
                    sp.wait_ge(s_tr, b - SLOTS + 1)
                    sp.dma_start(e8[:, b % SLOTS, :], e8_block(min(b * BLOCK, LAST_START))).then_inc(s_e8[b % SLOTS], 16)
            with sp.Else():
                sp.dma_start(e8[:, 0, :], e8_block(0)).then_inc(s_e8[0], 16)
                with sp.Fori(1, BLOCKS - 1) as b:
                    sp.wait_ge(s_tr, b + 0)
                    sp.dma_start(e8[:, 0, :], e8_block(b * BLOCK)).then_inc(s_e8[0], 16)
                sp.wait_ge(s_tr, BLOCKS - 1)
                sp.dma_start(e8[:, 0, :], e8_block(LAST_START)).then_inc(s_e8[0], 16)
            for n in range(len(STORES) - 1):
                j = slice(STORES[n], STORES[n + 1])
                sp.wait_ge(s_yr, STORES[n + 1])
                sp.dma_start(out_v[:, j, :], x_rows[:, j, :]).then_inc(s_out, 16)
            sp.wait_ge(s_out, 16 * (len(STORES) - 1))

        @block.gpsimd
        def _(pool):
            pool.memset(wfeat[:, :], 0.0).then_inc(s_zero_node, 1)
            pool.memset(wself_raw, 0.0).then_inc(s_zero_node, 1)
            pool.memset(ident[:, :], 0.0).then_inc(s_ident0, 1)
            pool.wait_ge(s_ident0, 1)
            pool.affine_select(out=ident[:, :], in_=ident[:, :], compare_op=ALU.not_equal, fill=1.0, base=0,
                               pattern=[[-1, 128]], channel_multiplier=1).then_inc(s_ident, 1)
            pool.memset(dst_rows[:, ROWS - 1, :], 0.0).then_inc(s_rows, 1)
            pool.memset(src_rows[:, ROWS - 1, :], 0.0).then_inc(s_rows, 1)
            pool.iota(iota_i[:, :], pattern=[[1, WINDOW]], base=0, channel_multiplier=0).then_inc(s_iota, 1)
            pool.memset(eps_col[:, :], EPS).then_inc(s_iota, 1)
            pool.memset(w1bd[:, :, :], 0.0).then_inc(s_zero, 1)
            pool.memset(w2bd[:, :], 0.0).then_inc(s_zero, 1)
            pool.memset(wpbd[:, :], 0.0).then_inc(s_zero, 1)
            pool.memset(conv_stage[:, :, :], 0.0).then_inc(s_zero, 1)
            pool.wait_ge(s_zero, 4)
            for to, of in loop_weights[:POOL_WEIGHT_LOADS]:
                pool.dma_start(to, of).then_inc(s_wts_pool, 16)
            for c in range(ROWS):
                pool.wait_ge(s_min, c + 1)
                pool.tensor_scalar(dst_rows[:, c, :], dst_rows.bitcast(INT32)[:, c, :], base_f[:, c:c + 1], None,
                                   ALU.subtract).then_inc(s_rel, 1)

            def gather(s, c):
                for t in range(CT * c, CT * (c + 1)):
                    pool.indirect_dma_start(out=gath[:, s, t, :], out_offset=None, in_=table[:, :],
                                            in_offset=bass.IndirectOffsetOnAxis(ap=idx[:, s, t:t + 1], axis=0))\
                        .then_inc(s_g[s][c], 16)

            def table_stored():
                for i in range(PIECE_SLOTS):
                    pool.wait_ge(s_tab[i], 16 * len(range(i, PIECES, PIECE_SLOTS)))

            table_stored()
            pool.wait_ge(s_flag, 1)
            flag = pool.value_load(flag_i[0:1, 0:1], min_val=0, max_val=NODES)
            with pool.If(flag < WINDOW):
                for b in range(SLOTS):
                    pool.wait_ge(s_idx, b + 1)
                    for c in range(CHUNKS):
                        gather(b, c)
                with pool.Fori(1, QUADS) as n:
                    for s in range(SLOTS):
                        pool.wait_ge(s_idx, n * SLOTS + (s + 1))
                        pool.sem_inc(s_round, 1)
                        for c in range(CHUNKS):
                            gather(s, c)
                for b in (BLOCKS - 2, BLOCKS - 1):
                    pool.wait_ge(s_idx, b + 1)
                    for c in range(CHUNKS):
                        if b < BLOCKS - 1 or c >= CUT // 2:
                            gather(b % SLOTS, c)
            with pool.Else():
                with pool.Fori(0, BLOCKS) as b:
                    pool.wait_ge(s_idx, b + 1)
                    pool.sem_inc(s_round, 1)
                    for c in range(CHUNKS):
                        gather(0, c)

        per_batch = -(-(LOOP_WEIGHT_LOADS - POOL_WEIGHT_LOADS) // (NODE_BATCHES - WEIGHTS_FROM))

        @block.scalar
        def _(act):
            act.wait_ge(s_zero_node, 2)
            act.dma_start(wfeat[0:MUL, 0:MUL], W1_0e[:, 0:MUL]).then_inc(s_node_w, 16)
            act.dma_start(wself_raw[0:MUL, 0:MUL], W1_0e[:, MUL:2 * MUL]).then_inc(s_node_w, 16)
            for i in range(3):
                cols = slice(MUL * (1 + i), MUL * (2 + i))
                act.dma_start(wfeat[MUL + i:128:3, cols], W1_1o[:, 0:MUL]).then_inc(s_node_w, 16)
                act.dma_start(wself_raw[MUL + i:128:3, cols], W1_1o[:, MUL:2 * MUL]).then_inc(s_node_w, 16)
            for n in range(NODE_BATCHES):
                if n == WEIGHTS_FROM:
                    act.wait_ge(s_zero, 4)
                if n >= WEIGHTS_FROM:
                    at = POOL_WEIGHT_LOADS + per_batch * (n - WEIGHTS_FROM)
                    for to, of in loop_weights[at:at + per_batch]:
                        act.dma_start(to, of).then_inc(s_wts_act, 16)
                act.wait_ge(s_xt, n + 1)
                act.copy(acc_v[:, :, BATCH * n:BATCH * (n + 1)].rearrange("q p j -> q j p"),
                         bank[n % 2][:, 0:BATCH * NODE_P].rearrange("q (j p) -> q j p", j=BATCH)).then_inc(s_xts, 1)

            def copy_indices(b, s):
                return act.copy(idx[:, s, :], src_all[:, bass.ds(b * TILES, TILES)])

            def copy_odd_indices():
                for c in range(1, ROWS, 2):
                    act.wait_ge(s_rt, c + 1)
                    for to, of in index_chunk(c):
                        act.copy(to, of).then_inc(s_rts[1], 1)
                act.wait_ge(s_rts[0], ROWS + 1)
                act.wait_ge(s_rts[1], ROWS - 1)

            def copy_attributes():
                for c in range(ROWS):
                    r = rows_of(c)
                    dest = ea_all[:, 1024 * c:1024 * c + 8 * r].rearrange("q (g e k) -> q e k g", e=2, k=4)
                    for e in range(2):
                        act.wait_ge(s_et, 2 * c + e + 1)
                        act.copy(dest[:, e], bank[6 + e][:, :].rearrange("q (k g) -> q k g", k=4)[:, :, 0:r])\
                            .then_inc(s_ets, 1)

            def gelu1(b, h):
                act.wait_ge(s_h1p[h], b + 1)
                act.activation(h1[:, h, :], hid_ps[h][:, :], ACT.Gelu_apprx_tanh,
                               scale=1.0 / math.sqrt(RADIAL)).then_inc(s_h1[h], 1)

            def gelu2(b, m, h):
                act.wait_ge(s_h2p[h], b + 1)
                act.activation(h2[:, m % 2, :, 4 * h:4 * (h + 1)].rearrange("p e a -> p a e"),
                               hid_ps[h][:, :].rearrange("p (a e) -> p a e", a=4), ACT.Gelu_apprx_tanh,
                               scale=1.0 / math.sqrt(HID)).then_inc(s_h2[h], 1)

            def copy_e8T(b):
                act.wait_ge(s_tr, b + 1)
                act.copy(e8T[:, :], t_ps).then_inc(s_e8T, 1)

            def copy_sums(b):
                act.wait_ge(s_seg[CHUNKS - 1], b + 1)
                act.copy(zsb[:, :], z_ps[:, :]).then_inc(s_zc, 1)

            def step(b, m, first=False, last=False):
                if not last:
                    copy_e8T(b + 1)
                    gelu1(b + 1, 0)
                    gelu1(b + 1, 1)
                if not first:
                    copy_sums(b - 1)
                if not last and not first:
                    copy_indices(b + (SLOTS - 1), (m + SLOTS - 1) % SLOTS).then_inc(s_idx, 1)
                if not last:
                    gelu2(b + 1, m + 1, 0)
                    gelu2(b + 1, m + 1, 1)

            act.wait_ge(s_flag, 1)
            flag = act.value_load(flag_i[0:1, 0:1], min_val=0, max_val=NODES)
            act.wait_ge(s_rts[0], 2)
            with act.If(flag < WINDOW):
                for b in range(SLOTS):
                    copy_indices(b, b).then_inc(s_idx, 1)
                copy_odd_indices()
                copy_attributes()
                copy_e8T(0)
                gelu1(0, 0)
                gelu1(0, 1)
                gelu2(0, 0, 0)
                gelu2(0, 0, 1)
                step(0, 0, first=True)
                with act.Fori(0, QUADS) as n:
                    for s in range(1, SLOTS + 1):
                        step(n * SLOTS + s, s)
                step(BLOCKS - 1, BLOCKS - 1, last=True)
                copy_sums(BLOCKS - 1)
            with act.Else():
                copy_odd_indices()
                copy_attributes()
                with act.Fori(0, BLOCKS) as b:
                    act.wait_ge(s_gblk, b + 1)
                    copy_indices(b, 0).then_inc(s_idx, 1)
                    copy_e8T(b)
                    gelu1(b, 0)
                    gelu1(b, 1)
                    gelu2(b, 0, 0)
                    gelu2(b, 0, 1)
                    for g in range(GROUPS):
                        act.wait_ge(s_gz, b * GROUPS + (g + 1))
                        for e in range(2):
                            last = act.copy(gen_z[:, e], bank[4 + e][:, :].rearrange("p (k n) -> p k n", k=4))
                        last.then_inc(s_gzc, 1)
            for n in range(NORM_BATCHES + 1):
                if n < NORM_BATCHES:
                    act.wait_ge(s_var, n + 1)
                    if n >= 4:
                        act.wait_ge(s_yr, NORM * (n - 3))
                    act.activation(rstd[0:NODE_P, n % 4, 0:norm_tiles(n), 0], moments[0:NODE_P, n % 4, 0:norm_tiles(n), 1],
                                   ACT.Sqrt, bias=eps_col[0:NODE_P, :]).then_inc(s_std, 1)
                if n >= 1:
                    act.wait_ge(s_sc, n)
                    for j in range(norm_tiles(n - 1)):
                        act.activation(x_rows[:, NORM * (n - 1) + j, :], norm_ps(n - 1, j), ACT.Identity,
                                       bias=rstd[0:NODE_P, (n - 1) % 4, j, 1:2],
                                       scale=rstd[0:NODE_P, (n - 1) % 4, j, 0:1]).then_inc(s_yr, 1)

        @block.tensor
        def _(pe):
            pe.wait_ge(s_ident, 1)
            def transpose_x(n):
                pe.wait_ge(s_x[next(i for i in range(len(LOADS)) if LOADS[i + 1] > BATCH * n)], 16)
                if n >= 2:
                    pe.wait_ge(s_xts, n - 1)
                for j in range(BATCH):
                    last = pe.transpose(bank[n % 2][:, NODE_P * j:NODE_P * (j + 1)], x_rows[:, BATCH * n + j, :],
                                        ident[0:NODE_P, 0:NODE_P])
                last.then_inc(s_xt, 1)

            def transpose_indices(c):
                r = rows_of(c)
                pe.wait_ge(s_rel, c + 1)
                pe.wait_ge(s_src_f, c + 1)
                if c >= 2:
                    pe.wait_ge(s_rts[c % 2], 2 * (c // 2))
                for k, rows in enumerate((src_rows, dst_rows)):
                    for e in range(2):
                        at = 256 * k + 128 * e
                        last = pe.transpose(bank[4 + c % 2][:, at:at + r], rows[0:r, c, e:256:2], ident[0:r, 0:r])
                last.then_inc(s_rt, 1)

            transpose_x(0)
            for n in range(NODE_BATCHES):
                if n + 1 < NODE_BATCHES:
                    transpose_x(n + 1)
                if n == 0:
                    pe.wait_ge(s_wnode, 3)
                pe.wait_ge(s_xts, n + 1)
                if n >= 2:
                    pe.wait_ge(s_feats, n - 1)
                for j in range(BATCH):
                    last = pe.matmul(bank[2 + n % 2][0:NODE_P, 128 * j:128 * (j + 1)], acc_v[:, :, BATCH * n + j],
                                     wfeat[:, :], start=True, stop=True)
                last.then_inc(s_featp, 1)
                if n == OFFSETS_FROM + ROWS:
                    pe.wait_ge(s_base, 1)
                    pe.transpose(bank[7][0:ROWS, 0:128], base_f[:, :], ident[:, :])
                    pe.transpose(bank[7][0:1, 128:256], relmax[:, ROWS:ROWS + 1], ident[:, :]).then_inc(s_small, 1)

            def init(n):
                if n >= 2:
                    pe.wait_ge(s_inits, n - 1)
                pe.matmul(bank[2 + n % 2][:, 0:INIT], winit[:, :], acc[:, INIT * n:INIT * (n + 1)],
                          start=True, stop=True).then_inc(s_initp, 1)

            transpose_indices(0)
            for n in range(EARLY_INITS):
                init(n)
            for c in range(1, ROWS):
                transpose_indices(c)
            for n in range(EARLY_INITS, NODE_BATCHES):
                init(n)
                for c in (c for c in range(ROWS) if attributes_behind(c) == n):
                    r = rows_of(c)
                    if c == 0:
                        pe.wait_ge(s_flag, 1)
                        pe.wait_ge(s_base13, 1)
                    pe.wait_ge(s_ea[c % EA_SLOTS], 16 * (c // EA_SLOTS + (1 if c < WHOLE else INDEX_LOADS)))
                    for e in range(2):
                        if c >= 1:
                            pe.wait_ge(s_ets, 2 * (c - 1) + e + 1)
                        for k in range(4):
                            last = pe.transpose(bank[6 + e][:, 128 * k:128 * k + r],
                                                ea_rows[0:r, c % EA_SLOTS, 4 * e + k:4 * GROUP:8], ident[0:r, 0:r])
                        last.then_inc(s_et, 1)
            pe.wait_ge(s_inits, NODE_BATCHES)
            pe.wait_ge(s_rts[0], ROWS + 1)
            pe.wait_ge(s_rts[1], ROWS - 1)
            pe.wait_ge(s_ets, 2 * ROWS)
            pe.wait_ge(s_flag, 1)
            pe.wait_ge(s_wts_pool, 16 * POOL_WEIGHT_LOADS)
            pe.wait_ge(s_wts_act, 16 * (LOOP_WEIGHT_LOADS - POOL_WEIGHT_LOADS))
            pe.wait_ge(s_conv, 3)

            def transpose_e8(s, round_, free=None):
                pe.wait_ge(s_e8[s], round_ * 16 + 16)
                if free is not None:
                    pe.wait_ge(s_h2[0], free)
                pe.transpose(t_ps, e8[:, s, :], ident[:, :]).then_inc(s_tr, 1)

            def layer1(b, h, free=None):
                if h == 0:
                    pe.wait_ge(s_e8T, b + 1)
                if free is not None:
                    pe.wait_ge(s_h2[h], free)
                for a in range(4 * h, 4 * h + 4):
                    last = pe.matmul(hid_ps[h][:, 128 * (a % 4):128 * (a % 4 + 1)], w1bd[:, a, :], e8T[:, :],
                                     start=True, stop=True)
                last.then_inc(s_h1p[h], 1)

            def layer2(b, h):
                pe.wait_ge(s_h1[h], b + 1)
                pe.matmul(hid_ps[h][:, :], w2bd[:, :], h1[:, h, :], start=True, stop=True).then_inc(s_h2p[h], 1)

            def radial(b, m, c, first=False):
                if c == 0:
                    pe.wait_ge(s_h2[0], b + 1)
                    pe.wait_ge(s_h2[1], b + 1)
                if not first:
                    pe.wait_ge(s_prod[c], b)
                for r in range(2):
                    g = 2 * c + r
                    last = pe.matmul(wgt_ps[c][:, 256 * r:256 * (r + 1)],
                                     h2[:, m % 2, 16 * g:16 * (g + 1), :].rearrange("p e a -> p (e a)"), wpbd[:, :],
                                     start=True, stop=True)
                last.then_inc(s_w[c], 1)

            def segment_sum(b, m, c, first=False):
                if c == 0:
                    pe.wait_ge(s_sel, b + 1)
                    if not first:
                        pe.wait_ge(s_zc, b + 0)
                pe.wait_ge(s_prod[c], b + 1)
                for r in range(2):
                    g = 2 * c + r
                    for half, at, n in ((0, 0, 1), (1, WINDOW, 3)):
                        o = 4 * WINDOW * g + at
                        for e in range(2):
                            last = pe.matmul(z_ps[:, o:o + n * WINDOW],
                                             prod[:, c, 2 * r + e, 128 * half:128 * (half + 1)],
                                             sel[:, m % 2, 2 * g + e, half:half + n, :], start=(e == 0), stop=(e == 1))
                last.then_inc(s_seg[c], 1)

            def convolve(b):
                pe.wait_ge(s_zc, b + 1)
                pe.wait_ge(s_add[GROUPS - 1], b + 1)
                for k in range(4):
                    last = pe.matmul(y_ps, conv[:, k, :],
                                     zsb[:, :].rearrange("p (g k w) -> p g k w", g=GROUPS, k=4)[:, :, k, :],
                                     start=(k == 0), stop=(k == 3))
                last.then_inc(s_y, 1)

            def step(b, m, round_, first=False, last=False):
                for c in range(CHUNKS):
                    if c == 0 and not last:
                        transpose_e8((m + 1) % SLOTS, round_, b + 1)
                    radial(b, m, c, first)
                    if not last:
                        if c < 2:
                            layer1(b + 1, c, b + 1)
                        else:
                            layer2(b + 1, c - 2)
                    if c >= 2:
                        segment_sum(b, m, c - 2, first)
                    elif not first:
                        segment_sum(b - 1, m - 1, c + 2)
                    if c == 2 and not first:
                        convolve(b - 1)

            flag = pe.value_load(flag_i[0:1, 0:1], min_val=0, max_val=NODES)
            with pe.If(flag < WINDOW):
                transpose_e8(0, 0)
                layer1(0, 0)
                layer1(0, 1)
                layer2(0, 0)
                layer2(0, 1)
                step(0, 0, 0, first=True)
                with pe.Fori(0, QUADS) as n:
                    for s in range(1, SLOTS + 1):
                        step(n * SLOTS + s, s, n + (s + 1) // SLOTS)
                step(BLOCKS - 1, BLOCKS - 1, 0, last=True)
                segment_sum(BLOCKS - 1, BLOCKS - 1, 2)
                segment_sum(BLOCKS - 1, BLOCKS - 1, 3)
                convolve(BLOCKS - 1)
                pe.wait_ge(s_add[GROUPS - 1], BLOCKS + 1)
            with pe.Else():
                with pe.Fori(0, BLOCKS) as b:
                    transpose_e8(0, b)
                    layer1(b, 0)
                    layer1(b, 1)
                    layer2(b, 0)
                    layer2(b, 1)
                    pe.wait_ge(s_h2[0], b + 1)
                    pe.wait_ge(s_h2[1], b + 1)
                    for g in range(GROUPS):
                        pe.wait_ge(s_gprod, b * GROUPS + (g + 1))
                        pe.matmul(wgt_ps[0][:, 0:256], h2[:, 0, 16 * g:16 * (g + 1), :].rearrange("p e a -> p (e a)"),
                                  wpbd[:, :], start=True, stop=True).then_inc(s_gw, 1)
                        pe.wait_ge(s_gdiag, b * GROUPS + (g + 1))
                        pe.wait_ge(s_gprod, b * GROUPS + (g + 2))
                        for e in range(2):
                            for half, n in ((0, 1), (1, 3)):
                                last = pe.matmul(bank[4 + e][:, 128 * half:128 * (half + n)],
                                                 prod[:, 0, e, 128 * half:128 * (half + 1)],
                                                 diag[:, e, half:half + n, :], start=True, stop=True)
                        last.then_inc(s_gz, 1)
                        pe.wait_ge(s_gzc, b * GROUPS + (g + 1))
                        for k in range(4):
                            last = pe.matmul(z_ps[:, 0:256], conv[:, k, :], gen_z[:, :, k, :],
                                             start=(k == 0), stop=(k == 3))
                        last.then_inc(s_gy, 1)
                    pe.wait_ge(s_gblk, b + 2)
            for n in range(NORM_BATCHES):
                if n >= 4:
                    pe.wait_ge(s_yr, NORM * (n - 3))
                for j in range(norm_tiles(n)):
                    last = pe.transpose(norm_ps(n, j), acc_v[:, :, NORM * n + j], ident[:, :])
                last.then_inc(s_ft, 1)

        @block.vector
        def _(dve):
            links = [0]

            def link(instruction):
                links[0] += 1
                instruction.then_inc(s_prep, 1)
                dve.wait_ge(s_prep, links[0])

            dve.wait_ge(s_node_w, 16 * NODE_WEIGHT_LOADS)
            dve.wait_ge(s_ident, 1)
            dve.tensor_scalar(wfeat[:, :], wfeat[:, :], FEAT_SCALE, None, ALU.mult).then_inc(s_wnode, 1)
            dve.scalar_tensor_tensor(winit[:, 0:MUL], wself_raw[:, 0:MUL], SELF_SCALE, ident[:, 0:MUL],
                                     ALU.mult, ALU.add).then_inc(s_wnode, 1)
            by_unit = lambda ap: ap.rearrange("p (w i) -> p i w", i=3)
            dve.scalar_tensor_tensor(by_unit(winit[:, MUL:128]), wself_raw[:, MUL:128].rearrange("p (i w) -> p i w", i=3),
                                     SELF_SCALE, by_unit(ident[:, MUL:128]), ALU.mult, ALU.add).then_inc(s_wnode, 1)
            dve.wait_ge(s_iota, 2)
            dve.tensor_copy(iota_w[:, :], iota_i[:, :]).then_inc(s_wnode, 1)
            dve.memset(src_all[:, ALL_GROUPS * 2:], 0).then_inc(s_wnode, 1)
            dve.memset(acc[:, NODES:], 0.0).then_inc(s_wnode, 1)

            dst_i, src_i = dst_rows.bitcast(INT32), src_rows.bitcast(INT32)

            def copy_even_indices(c):
                dve.wait_ge(s_rt, c + 1)
                for to, of in index_chunk(c):
                    dve.tensor_copy(to, of).then_inc(s_rts[0], 1)

            def copy_init(n):
                dve.wait_ge(s_initp, n + 1)
                dve.tensor_copy(acc[:, INIT * n:INIT * (n + 1)], bank[2 + n % 2][:, 0:INIT]).then_inc(s_inits, 1)

            def extremes(c):
                dve.tensor_reduce(relmax[:, c:c + 1], dst_i[:, c, :], AXIS_X, ALU.max)
                dve.tensor_reduce(base_f[:, c:c + 1], dst_i[:, c, :], AXIS_X, ALU.min).then_inc(s_min, 1)

            for n in range(NODE_BATCHES):
                piece = next(i for i in range(PIECES) if TABLE_CUTS[i + 1] > BATCH * n)
                j = BATCH * n - TABLE_CUTS[piece]
                dve.wait_ge(s_featp, n + 1)
                if j == 0 and piece >= PIECE_SLOTS:
                    dve.wait_ge(s_tab[piece % PIECE_SLOTS], 16 * (piece // PIECE_SLOTS))
                dve.tensor_copy(feat_rows[:, piece % PIECE_SLOTS, j:j + BATCH, :],
                                bank[2 + n % 2][0:NODE_P, :].rearrange("p (j f) -> p j f", j=BATCH)).then_inc(s_feats, 1)
                if OFFSETS_FROM <= n < OFFSETS_FROM + ROWS:
                    if n == OFFSETS_FROM:
                        dve.wait_ge(s_dst, 16 * INDEX_LOADS)
                    extremes(n - OFFSETS_FROM)
                if n == OFFSETS_FROM + ROWS - 1:
                    dve.wait_ge(s_min, ROWS)
                    link(dve.tensor_tensor(relmax[:, 0:ROWS], relmax[:, 0:ROWS], base_f[:, :], ALU.subtract))
                    dve.tensor_reduce(relmax[:, ROWS:ROWS + 1], relmax[:, 0:ROWS], AXIS_X, ALU.max).then_inc(s_base, 1)
                if n == OFFSETS_FROM + ROWS + 2:
                    dve.wait_ge(s_small, 1)
                    dve.tensor_reduce(flag_i[0:1, 0:1], bank[7][0:1, 128:256], AXIS_X, ALU.max).then_inc(s_flag, 1)
                    dve.tensor_copy(base13[:, :], bank[7][0:ROWS, 0:128]).then_inc(s_base13, 1)
            for c in range(ROWS):
                if c == 0:
                    dve.wait_ge(s_src0, 16)
                if c == 1:
                    dve.wait_ge(s_src, 16 * INDEX_LOADS)
                dve.tensor_copy(src_rows[:, c, :], src_i[:, c, :]).then_inc(s_src_f, 1)
                if c == 0:
                    copy_even_indices(0)
                    for n in range(EARLY_INITS):
                        copy_init(n)
            for c in range(2, ROWS, 2):
                copy_even_indices(c)
            for n in range(EARLY_INITS, NODE_BATCHES):
                copy_init(n)
                if n == attributes_behind(ROWS - EA_SLOTS - 1) + 1:
                    dve.wait_ge(s_et, 2 * (ROWS - EA_SLOTS))
                    dve.memset(ea_rows[:, (ROWS - 1) % EA_SLOTS, :], 0.0).then_inc(s_eaz, 1)
            dve.wait_ge(s_wts_pool, 16 * POOL_WEIGHT_LOADS)
            dve.wait_ge(s_wts_act, 16 * (LOOP_WEIGHT_LOADS - POOL_WEIGHT_LOADS))
            dve.tensor_scalar(conv[:, :, MUL:128].rearrange("p k (w i) -> p k i w", i=3),
                              conv_stage[:, :, MUL:128].rearrange("p k (i w) -> p k i w", i=3),
                              CONV_SCALE, None, ALU.mult).then_inc(s_conv, 1)
            dve.tensor_scalar(conv[:, 0, 0:MUL], conv_stage[:, 0, 0:MUL], CONV_SCALE, None, ALU.mult).then_inc(s_conv, 1)
            dve.tensor_scalar(conv[:, 1:4, 0:MUL], conv_stage[:, 1:4, 0:MUL], CONV_SCALE * INV_SQRT3, None,
                              ALU.mult).then_inc(s_conv, 1)
            dve.wait_ge(s_ets, 2 * ROWS)
            dve.wait_ge(s_inits, NODE_BATCHES)

            def select(b, m, free=None):
                ts_ = bass.ds(b * TILES, TILES)
                if free is not None:
                    dve.wait_ge(s_seg[CHUNKS - 1], free)
                dve.wait_ge(s_sel, b + 0)
                dve.tensor_tensor(sel01[:, :, :], rel_all[:, ts_].unsqueeze(2).to_broadcast([128, TILES, WINDOW]),
                                  iota_w[:, :].unsqueeze(1).to_broadcast([128, TILES, WINDOW]),
                                  ALU.is_equal).then_inc(s_sel0, 1)
                dve.wait_ge(s_sel0, b + 1)
                attr = ea_all[:, bass.ds(b * (TILES * 4), TILES * 4)].rearrange("q (t k) -> q t k", k=4)
                dve.tensor_tensor(sel[:, m % 2], sel01[:, :, :].unsqueeze(2).to_broadcast([128, TILES, 4, WINDOW]),
                                  attr.unsqueeze(3).to_broadcast([128, TILES, 4, WINDOW]), ALU.mult).then_inc(s_sel, 1)

            def multiply(weights, rows, to, n):
                w = weights.rearrange("q (t h a u) -> q t h a u", t=n, h=2, a=2)
                f = rows.rearrange("q t (s u) -> q t s u", s=4)
                o = to.rearrange("q t (h s u) -> q t h s u", h=2, s=4)
                dve.tensor_tensor(o[:, :, :, 0, :], w[:, :, :, 0, :],
                                  f[:, :, 0, :].unsqueeze(2).to_broadcast([128, n, 2, MUL]), ALU.mult)
                for h in range(2):
                    last = dve.tensor_tensor(o[:, :, h, 1:4, :],
                                             w[:, :, h, 1, :].unsqueeze(2).to_broadcast([128, n, 3, MUL]),
                                             f[:, :, 1:4, :], ALU.mult)
                return last

            def products(b, m, c, round_, first=False):
                dve.wait_ge(s_w[c], b + 1)
                dve.wait_ge(s_g[m % SLOTS][c], round_ * (16 * CT) + 16 * CT)
                if not first:
                    dve.wait_ge(s_seg[c], b)
                multiply(wgt_ps[c][:, :], gath[:, m % SLOTS, CT * c:CT * (c + 1), :], prod[:, c], CT).then_inc(s_prod[c], 1)

            def add_windows(b):
                _, base = nc.values_load_multi_w_load_instructions(
                    base_row[0:1, bass.ds(b * GROUPS, GROUPS)], engines=(mybir.EngineType.DVE,),
                    min_val=0, max_val=NODES - 1,
                    skip_runtime_bounds_check_because="a destination is a node's number by the kernel's contract")
                dve.wait_ge(s_y, b + 1)
                for g in range(GROUPS):
                    dve.wait_ge(s_add[g - 1], b + 1)
                    at = bass.ds(base[g], WINDOW)
                    dve.tensor_tensor(acc[:, at], acc[:, at], y_ps[:, WINDOW * g:WINDOW * (g + 1)], ALU.add)\
                        .then_inc(s_add[g], 1)

            def step(b, m, round_, first=False, last=False):
                for c in range(CHUNKS):
                    if c == 2 and not last:
                        select(b + 1, m + 1, None if first else b)
                    products(b, m, c, round_ - (last and c < CUT // 2), first)
                if not first:
                    add_windows(b - 1)

            flag = dve.value_load(flag_i[0:1, 0:1], min_val=0, max_val=NODES)
            dve.wait_ge(s_br, 16)
            with dve.If(flag < WINDOW):
                dve.sem_inc(s_add[GROUPS - 1], 1)
                select(0, 0)
                step(0, 0, 0, first=True)
                with dve.Fori(0, QUADS) as n:
                    for s in range(1, SLOTS + 1):
                        step(n * SLOTS + s, s, n + s // SLOTS)
                step(BLOCKS - 1, BLOCKS - 1, (BLOCKS - 1) // SLOTS, last=True)
                add_windows(BLOCKS - 1)
            with dve.Else():
                dve.sem_inc(s_gprod, 1)
                dve.sem_inc(s_gblk, 1)

                def general_block(b, start):
                    for c in range(CHUNKS):
                        dve.wait_ge(s_g[0][c], b * (16 * CT) + 16 * CT)
                    for g in range(GROUPS):
                        for e in range(2):
                            attr = ea_all[:, bass.ds(b * (TILES * 4) + 4 * (2 * g + e), 4)]
                            last = dve.tensor_tensor(diag[:, e], ident[:, :].unsqueeze(1).to_broadcast([128, 4, 128]),
                                                     attr.unsqueeze(2).to_broadcast([128, 4, 128]), ALU.mult)
                        last.then_inc(s_gdiag, 1)
                        dve.wait_ge(s_gw, b * GROUPS + (g + 1))
                        multiply(wgt_ps[0][:, 0:256], gath[:, 0, 2 * g:2 * g + 2, :], prod[:, 0, 0:2], 2)\
                            .then_inc(s_gprod, 1)
                        columns = z_ps[:, 0:256].rearrange("f (e n) -> f n e", e=2)
                        dve.sem_clear(s_gadd)
                        dve.sem_inc(s_gadd, 1)
                        with dve.Fori(0, GROUP // 4) as n:
                            _, node = nc.values_load_multi_w_load_instructions(
                                dst[bass.ds(start + GROUP * g + n * 4, 4)].rearrange("(a n) -> a n", a=1),
                                engines=(mybir.EngineType.DVE,), min_val=0, max_val=NODES - 1)
                            dve.wait_ge(s_gy, b * GROUPS + (g + 1))
                            for k in range(4):
                                dve.wait_ge(s_gadd, n * 4 + (k + 1))
                                at = bass.ds(node[k], 1)
                                dve.tensor_tensor(acc[:, at], acc[:, at], columns[:, bass.ds(n * 2 + k // 2, 1), k % 2],
                                                  ALU.add).then_inc(s_gadd, 1)
                        dve.wait_ge(s_gadd, GROUP + 1)
                    dve.memset(flag_i[0:1, 1:2], 0).then_inc(s_gblk, 1)

                with dve.Fori(0, BLOCKS - 1) as b:
                    general_block(b, b * BLOCK)
                general_block(BLOCKS - 1, LAST_START)

            def moments_of(n):
                dve.wait_ge(s_ft, n + 1)
                for j in range(norm_tiles(n)):
                    last = dve.bn_stats(stats[0:NODE_P, n % 4, j, :], norm_ps(n, j))
                link(last)
                for j in range(norm_tiles(n)):
                    last = dve.bn_aggr(moments[0:NODE_P, n % 4, j, :], stats[0:NODE_P, n % 4, j, :])
                last.then_inc(s_var, 1)

            def scales_of(n):
                dve.wait_ge(s_std, n + 1)
                r = rstd[0:NODE_P, n % 4, 0:norm_tiles(n), :]
                link(dve.reciprocal(r[:, :, 0], r[:, :, 0]))
                dve.scalar_tensor_tensor(r[:, :, 1], moments[0:NODE_P, n % 4, 0:norm_tiles(n), 0], -1.0, r[:, :, 0],
                                         ALU.mult, ALU.mult).then_inc(s_sc, 1)

            for n in range(NORM_BATCHES + 1):
                if n < NORM_BATCHES:
                    moments_of(n)
                if n >= 1:
                    scales_of(n - 1)
    return nc


_INS = ['x', 'src', 'dst', 'edge_attr_4', 'edge_attr_8', 'L0_gnn_W1_0e', 'L0_gnn_W1_1o', 'L0_gnn_W_mlp1',
        'L0_gnn_W_mlp2', 'L0_gnn_Wp_00', 'L0_gnn_Wp_01', 'L0_gnn_Wp_10', 'L0_gnn_Wp_11', 'L0_gnn_W2_0e', 'L0_gnn_W2_1o']


def kernel(**inputs):
    import numpy as np
    import concourse.bacc as bacc
    from concourse.bass_utils import run_bass_kernel_spmd

    nc = bacc.Bacc("TRN2", target_bir_lowering=False, num_devices=1)
    arrays, aps = {}, {}
    for name in _INS:
        a = np.ascontiguousarray(inputs[name])
        arrays[f"in_{name}"] = a
        aps[name] = nc.dram_tensor(f"in_{name}", a.shape, mybir.dt.from_np(a.dtype), kind="ExternalInput").ap()
    out = nc.dram_tensor("out_0", (NODES, FEAT), FP32, kind="ExternalOutput").ap()
    w = {name.removeprefix("L0_gnn_"): aps[name] for name in _INS[5:]}
    build_program(nc, aps['x'], aps['src'], aps['dst'], aps['edge_attr_4'], aps['edge_attr_8'], w['W1_0e'], w['W1_1o'],
                  w['W_mlp1'], w['W_mlp2'], [w['Wp_00'], w['Wp_10'], w['Wp_01'], w['Wp_11']], w['W2_0e'], w['W2_1o'], out)
    r = run_bass_kernel_spmd(nc, [arrays], core_ids=[0])
    return r.results[0]["out_0"]
```
